# Optimizing a Trainium2 kernel written in Bass

```python
import numpy as np
import jax
import jax.numpy as jnp

def _softmax(x, axis=-1):
    return jax.nn.softmax(x, axis=axis)

def _gelu(x):
    return jax.nn.gelu(x, approximate=True)

def _silu(x):
    return jax.nn.silu(x)

def _sigmoid(x):
    return jax.nn.sigmoid(x)

def _layernorm(x, axis=-1, eps=1e-05):
    m = jnp.mean(x, axis=axis, keepdims=True)
    v = jnp.var(x, axis=axis, keepdims=True)
    return (x - m) / jnp.sqrt(v + eps)

def _scatter_add(tgt, idx, src, axis=0):
    return tgt.at[idx].add(src)

def _segment_sum(src, seg, n):
    return jax.ops.segment_sum(src, seg, n)
kernel_name = 'mk_gnn_resnorm_d2_gnn_r64_81a1bb'

def setup_inputs(seed: int=0):
    np.random.seed(seed)
    _w = jnp.asarray

    def _rec_inputs():
        import jax
        import jax.numpy as jnp
        _gk = jax.random.key(seed)
        x = 0.0003989 + 1 * jax.random.normal(jax.random.fold_in(_gk, 1), (50000, 128), jnp.float32)
        src = jax.random.randint(jax.random.fold_in(_gk, 2), (25000,), 0, 50000, jnp.int32)
        dst = jax.random.randint(jax.random.fold_in(_gk, 3), (25000,), 0, 50000, jnp.int32)
        _o = jnp.argsort(dst, stable=True)
        src = src[_o]
        dst = dst[_o]
        edge_type_9 = jax.random.randint(jax.random.fold_in(_gk, 12), (25000,), 0, 9, jnp.int32)
        return (x, src, dst, edge_type_9)
    x, src, dst, edge_type_9 = _rec_inputs()

    def _L0_gnn_setup():
        import jax, jax.numpy as jnp
        import numpy as np
        N_NODES = 50000
        EMB = 128
        N_REL = 9
        N_EDGES = 12500
        N_LAYERS = 2
        key = jax.random.key(seed)
        k1, k2, k3, k4, k5 = jax.random.split(key, 5)
        edge_index = jax.random.randint(k1, (2, N_EDGES), 0, N_NODES)
        edge_type = jax.random.randint(k2, (N_EDGES,), 0, N_REL)
        embeddings = jax.random.normal(k3, (N_NODES, EMB), dtype=jnp.float32)
        rgcn_weights = jax.random.uniform(k4, (N_LAYERS, 2 * N_REL + 1, EMB, EMB), dtype=jnp.float32) * 0.02
        rgcn_biases = jax.random.uniform(k5, (N_LAYERS, 2 * N_REL + 1, EMB), dtype=jnp.float32) * 0.02
        return {'edge_index': edge_index, 'edge_type': edge_type, 'embeddings': embeddings, 'rgcn_weights': rgcn_weights, 'rgcn_biases': rgcn_biases}
    _L0_gnn_all = _L0_gnn_setup()
    _L0_gnn_in = {k: v for k, v in _L0_gnn_all.items() if k in ('rgcn_weights', 'rgcn_biases')}
    del _L0_gnn_all

    def _L1_gnn_setup():
        import jax, jax.numpy as jnp
        import numpy as np
        N = 50000
        D = 128
        E = 9375

        def _gcn_conv(x, src, dst, W, b):
            n = x.shape[0]
            deg = jax.ops.segment_sum(jnp.ones_like(dst, dtype=x.dtype), dst, num_segments=n)
            dinv = jnp.where(deg > 0, jax.lax.rsqrt(deg), 0.0)
            norm = dinv[src] * dinv[dst]
            h = x @ W
            msg = h[src] * norm[:, None]
            out = jax.ops.segment_sum(msg, dst, num_segments=n)
            return out + b
        key = jax.random.key(seed)
        k1, k2, k3, k4, k5, k6 = jax.random.split(key, 6)
        x = jax.random.normal(k1, (N, D), dtype=jnp.float32)
        edge_index = jax.random.randint(k2, (2, E), 0, N, dtype=jnp.int32)
        s = 1.0 / np.sqrt(D)
        W1 = jax.random.uniform(k3, (D, D), dtype=jnp.float32, minval=-s, maxval=s)
        b1 = jax.random.uniform(k4, (D,), dtype=jnp.float32, minval=-s, maxval=s)
        W2 = jax.random.uniform(k5, (D, D), dtype=jnp.float32, minval=-s, maxval=s)
        b2 = jax.random.uniform(k6, (D,), dtype=jnp.float32, minval=-s, maxval=s)
        return {'x': x, 'edge_index': edge_index, 'W1': W1, 'b1': b1, 'W2': W2, 'b2': b2}
    _L1_gnn_all = _L1_gnn_setup()
    _L1_gnn_in = {k: v for k, v in _L1_gnn_all.items() if k in ('W1', 'b1', 'W2', 'b2')}
    del _L1_gnn_all
    return {'x': x, 'src': src, 'dst': dst, 'edge_type_9': edge_type_9, 'L0_gnn_rgcn_weights': _L0_gnn_in['rgcn_weights'], 'L0_gnn_rgcn_biases': _L0_gnn_in['rgcn_biases'], 'L1_gnn_W1': _L1_gnn_in['W1'], 'L1_gnn_b1': _L1_gnn_in['b1'], 'L1_gnn_W2': _L1_gnn_in['W2'], 'L1_gnn_b2': _L1_gnn_in['b2']}

def reference(x, src, dst, edge_type_9, L0_gnn_rgcn_weights, L0_gnn_rgcn_biases, L1_gnn_W1, L1_gnn_b1, L1_gnn_W2, L1_gnn_b2):
    import jax
    import jax.numpy as jnp

    def _L0_gnn_ref(edge_index, edge_type, embeddings, rgcn_weights, rgcn_biases):
        import jax, jax.numpy as jnp
        import numpy as np
        N_NODES = 50000
        EMB = 128
        N_REL = 9
        N_EDGES = 12500
        N_LAYERS = 2
        n = embeddings.shape[0]
        R = N_REL
        seg = jnp.concatenate([edge_type * n + edge_index[0], (edge_type + R) * n + edge_index[1]])
        srcs = jnp.concatenate([edge_index[1], edge_index[0]])
        ones = jnp.ones(seg.shape, embeddings.dtype)
        count = jax.ops.segment_sum(ones, seg, num_segments=2 * R * n).reshape(2 * R, n, 1)
        cnt = jnp.maximum(count, 1.0)
        output = embeddings
        for l in range(N_LAYERS):
            W, b = (rgcn_weights[l], rgcn_biases[l])
            agg = jax.ops.segment_sum(output[srcs], seg, num_segments=2 * R * n)
            agg = agg.reshape(2 * R, n, -1)
            hidden = output @ W[-1] + b[-1]
            for r in range(R):
                for inv in (0, 1):
                    s = r + R * inv
                    msum = agg[s] @ W[s] + count[s] * b[s]
                    hidden = 2.0 * (hidden + msum) / cnt[s]
            if l + 1 < N_LAYERS:
                hidden = jax.nn.relu(hidden)
            output = hidden
        return output

    def _L1_gnn_ref(x, edge_index, W1, b1, W2, b2):
        import jax, jax.numpy as jnp
        import numpy as np
        N = 50000
        D = 128
        E = 9375

        def _gcn_conv(x, src, dst, W, b):
            n = x.shape[0]
            deg = jax.ops.segment_sum(jnp.ones_like(dst, dtype=x.dtype), dst, num_segments=n)
            dinv = jnp.where(deg > 0, jax.lax.rsqrt(deg), 0.0)
            norm = dinv[src] * dinv[dst]
            h = x @ W
            msg = h[src] * norm[:, None]
            out = jax.ops.segment_sum(msg, dst, num_segments=n)
            return out + b
        n = x.shape[0]
        loops = jnp.arange(n, dtype=edge_index.dtype)
        src = jnp.concatenate([edge_index[0], loops])
        dst = jnp.concatenate([edge_index[1], loops])
        h = jax.nn.relu(_gcn_conv(x, src, dst, W1, b1))
        out = jax.nn.relu(_gcn_conv(h, src, dst, W2, b2))
        return out
    edge_index = jnp.stack([src, dst])
    x = _layernorm(x + _L0_gnn_ref(edge_index, edge_type_9, x, L0_gnn_rgcn_weights, L0_gnn_rgcn_biases), axis=-1)
    x = _layernorm(x + _L1_gnn_ref(x, edge_index, L1_gnn_W1, L1_gnn_b1, L1_gnn_W2, L1_gnn_b2), axis=-1)
    return x

_drawn_inputs = setup_inputs


def setup_inputs(seed=0):
    import zlib

    import numpy as np

    out = dict(_drawn_inputs(seed))
    spreads = {}
    factors = {'L1_gnn_b1': 3.886}
    for name, (base, spread) in spreads.items():
        noise = np.random.default_rng([zlib.crc32(name.encode()), seed]).standard_normal(out[name].shape)
        drawn = base * np.exp(spread * noise) if base else spread * noise
        out[name] = jnp.asarray(drawn.astype(out[name].dtype))
    for name, factor in factors.items():
        out[name] = (out[name] * factor).astype(out[name].dtype)
    return out
```

```python
import concourse.bass as bass
from concourse import mybir
from contextlib import ExitStack

FP32 = mybir.dt.float32
BF16 = mybir.dt.bfloat16
FP16 = mybir.dt.float16
I32 = mybir.dt.int32
ALU = mybir.AluOpType
ACT = mybir.ActivationFunctionType
AX = mybir.AxisListType

P = 128
D = 128
STRIP = 512
NB = STRIP // P
R = 9
TRI = 3
NG = R // TRI
KK = 2 * R
RING = 8
UNROLL = 16
EPS = 1e-5
FAR = 4096


class Shapes:

    def __init__(self, n, e):
        self.N, self.E = n, e
        self.NST = -(-n // STRIP)
        self.LAST = n - (self.NST - 1) * STRIP
        self.COLS = -(-(-(-e // P)) // 14) * 14
        assert self.COLS * P - e < P and self.COLS <= 256
        msg_tiles = -(-2 * e // P)
        self.BINS = self.NST * 2 * NG
        self.DBINS = self.NST * NG
        self.NT = -(-(msg_tiles + self.BINS + 2 + UNROLL + 2) // P) * P
        self.NTG = -(-(-(-e // P) + self.DBINS + UNROLL + 2) // P) * P


def rows_of(ap, strips):
    return ap.rearrange("(s p b) d -> s p (b d)", p=P, b=NB) if strips else ap


def col(t, i, n=1):
    return t[:, bass.ds(i, n)]


def within(value, most):
    return value.with_bounds(min_val=0, max_val=most)


def clear(nc, sems):
    with nc.Block() as block:
        @block.sync
        def _(sp):
            for s in sems:
                sp.sem_clear(s)


def build_tables(nc, sh, sb, src, dst, etype, dram, res):
    NST, COLS, NT, DB = sh.NST, sh.COLS, sh.NT, sh.DBINS
    NTC, NGC = sh.NT // P, sh.NTG // P
    GRP = 7
    GROUPS = COLS // GRP
    full, rest = sh.E // COLS, sh.E % COLS
    iota, ident = res["iota"], res["ident"]

    sems = []
    with ExitStack() as ctx:
        def t(name, shape, dt=FP32):
            return ctx.enter_context(nc.sbuf_tensor("s_" + name, shape, dt))

        def sem(name):
            sems.append(ctx.enter_context(nc.semaphore("s_" + name)))
            return sems[-1]

        raw = t("raw", [P, 3, COLS], I32)
        ones = t("ones", [P, P], FP16)
        zero = t("zero", [P, 512], FP16)
        before = t("before", [P, P], FP16)
        row0 = t("row0", [P, P], FP16)
        sums = t("sums", [P, 2, 2, DB + 1], FP16)
        ints = t("ints", [P, 8, COLS], I32)
        flts = t("flts", [P, 8, COLS])
        key = t("key", [P, 2, COLS])
        rec = t("rec", [P, 2, COLS, 4], I32)
        onehot = t("onehot", [P, 2, 2, GRP, DB + 1], FP16)
        cnt = t("cnt", [P, NST, 2, NG])
        cnti = t("cnti", [P, NST, 2, NG], I32)
        tiles = t("tiles", [P, NST, 2, NG])
        incl = t("incl", [P, sh.BINS])
        ts = t("ts", [P, sh.BINS + 1])
        onesrow = t("onesrow", [P, sh.BINS])
        start = t("start", [P, 2, DB + 1], FP16)
        wmod = t("wmod", [P, sh.BINS])
        gcnt = t("gcnt", [P, NST])
        gincl = t("gincl", [P, NST])
        gs = t("gs", [P, NST + 1])
        toti = t("toti", [P, 4], I32)
        junk = t("junk", [P, sh.BINS])
        junk2 = t("junk2", [P, 2, 2, DB + 1])
        tno = t("tno", [P, NTC])
        pt = t("pt", [P, 5, NTC])
        pti = t("pti", [P, 5, NTC], I32)
        posf = t("posf", [P, 2, 2, GRP])
        posi = t("posi", [P, 2, 3, 2 * GRP], I32)
        rows = t("rows", [P, 2, 2 * GRP], I32)
        recs = t("recs", [P, 2, 2 * GRP, 4], I32)
        fill = t("fill", [P, NT, 4], I32)
        ps_cnt = [ctx.enter_context(nc.psum_tensor(f"s_ps_cnt{d}", [P, 512], FP32)) for d in range(2)]
        ps_pos = [ctx.enter_context(nc.psum_tensor(f"s_ps_pos{d}", [P, 2, 512], FP32)) for d in range(2)]

        raw_cleared, raw_in = sem("raw_cleared"), sem("raw_in")
        consts, fill_ready, filled = sem("consts"), sem("fill_ready"), sem("filled")
        chain, hot_ready, hist_done = sem("chain"), sem("hot_ready"), sem("hist_done")
        base_ready, hot2_ready = sem("base_ready"), [sem("hot2_ready0"), sem("hot2_ready1")]
        pos_ready, pos_read = [sem("pos_ready0"), sem("pos_ready1")], [sem("pos_read0"), sem("pos_read1")]
        staged, scattered = sem("staged"), res["landed"]["s"]
        sums_ready = [sem("sums_ready0"), sem("sums_ready1")]
        gate, stage_free = sem("gate"), sem("stage_free")
        chain2, tiles_ready, tiles_out = sem("chain2"), sem("tiles_ready"), sem("tiles_out")
        tab_in, row_in = sem("tab_in"), sem("row_in")

        with nc.Block() as block:
            @block.sync
            def _(sp):
                sp.wait_ge(raw_cleared, 1)
                for i, a in enumerate((src, dst, etype)):
                    sp.dma_start(raw[0:full, i, :], a[0:full * COLS].rearrange("(p c) -> p c", c=COLS)).then_inc(raw_in, 16)
                    if rest:
                        sp.dma_start(raw[full:full + 1, i, 0:rest],
                                     a[full * COLS:sh.E].rearrange("(p c) -> p c", p=1)).then_inc(raw_in, 16)
                sp.wait_ge(fill_ready, 2)
                sp.dma_start(dram["table"].rearrange("(p t) w -> p (t w)", p=P),
                             fill[:, :, :].rearrange("p t w -> p (t w)")).then_inc(filled, 16)
                sp.wait_ge(tiles_ready, 1)
                with nc.allow_non_contiguous_dma(reason="a few hundred words, once"):
                    for i in range(5):
                        sp.dma_start(dram["bytile"][i, :].rearrange("(c p) -> p c", p=P), pti[:, i, :]).then_inc(tiles_out, 16)
                sp.wait_ge(tiles_out, 80)
                sp.dma_start(res["bytile"][:, :], dram["bytile"].rearrange("(o a) t -> o (a t)", o=1)).then_inc(row_in, 16)
                sp.wait_ge(row_in, 16)
                for h in range(2):
                    sp.wait_ge(scattered[h], 16 * 2 * GRP * (GROUPS // 2))
                sp.wait_ge(filled, 16)
                sp.dma_start(res["tab"][:, :, :].rearrange("p t w -> p (t w)"),
                             dram["table"].rearrange("(p t) w -> p (t w)", p=P)).then_inc(tab_in, 16)
                sp.wait_ge(tab_in, 16)

            @block.gpsimd
            def _(pool):
                nc.gpsimd.memset(before[:, :], 1.0).then_inc(consts, 1)
                nc.gpsimd.memset(row0[:, :], float(P)).then_inc(consts, 1)
                nc.gpsimd.memset(ident[:, :], 0.0).then_inc(consts, 1)
                nc.gpsimd.iota(iota[:, :], pattern=[[1, STRIP]], base=0, channel_multiplier=0,
                               allow_small_or_imprecise_dtypes=True).then_inc(consts, 1)
                nc.gpsimd.iota(tno[:, :], pattern=[[P, NTC]], base=0, channel_multiplier=1,
                               allow_small_or_imprecise_dtypes=True).then_inc(consts, 1)
                pool.wait_ge(consts, 5)
                nc.gpsimd.affine_select(out=before[:, :], in_=before[:, :], compare_op=ALU.is_gt, fill=0.0, base=0,
                                        pattern=[[1, P]], channel_multiplier=-1).then_inc(consts, 1)
                nc.gpsimd.affine_select(out=row0[:, :], in_=row0[:, :], compare_op=ALU.is_equal, fill=0.0, base=0,
                                        pattern=[[0, P]], channel_multiplier=1).then_inc(consts, 1)
                nc.gpsimd.affine_select(out=ident[:, :], in_=ident[:, :], compare_op=ALU.not_equal, fill=1.0, base=0,
                                        pattern=[[1, P]], channel_multiplier=-1).then_inc(consts, 1)
                nc.gpsimd.memset(fill[:, :, :], -1).then_inc(fill_ready, 1)
                pool.wait_ge(fill_ready, 1)
                nc.gpsimd.memset(fill[:, :, 0:1], 0).then_inc(fill_ready, 1)
                pool.wait_ge(filled, 16)
                with pool.Fori(0, GROUPS // 2) as i:
                    for h in range(2):
                        pool.wait_ge(staged, i * 2 + (h + 1))
                        pool.sem_inc(gate, 1)
                        for c in range(2 * GRP):
                            nc.gpsimd.indirect_dma_start(
                                dram["table"], bass.IndirectOffsetOnAxis(ap=rows[:, h, c:c + 1], axis=0),
                                recs[:, h, c, :], None).then_inc(scattered[h], 16)
                    for h in range(2):
                        pool.wait_ge(scattered[h], (i + 1) * (16 * 2 * GRP))
                        pool.sem_inc(stage_free, 1)

            @block.vector
            def _(v):
                n = [0]

                def link(ins):
                    n[0] += 1
                    ins.then_inc(chain, 1)
                    v.wait_ge(chain, n[0])

                V = nc.vector
                V.memset(zero[:, :], 0.0)
                V.memset(ones[:, :], 1.0)
                V.memset(sums[:, :, 0, :], 0.0)
                V.memset(onesrow[:, :], 1.0)
                link(V.memset(wmod[:, :], 1.0))
                link(V.memset(wmod[:, :].rearrange("p (s g) -> p s g", g=2 * NG)[:, :, 0:1], -float(2 * NG - 1)))
                link(V.memset(wmod[:, 0:1], 0.0))
                link(V.memset(raw[:, 0:2, :], NST * STRIP))
                V.memset(raw[:, 2, :], 0).then_inc(raw_cleared, 1)
                v.wait_ge(raw_in, 48 * (2 if rest else 1))
                v.wait_ge(consts, 8)
                ty, tg, rel3, a, b, pad, stf = (flts[:, k, :] for k in range(7))
                link(V.tensor_copy(ty, raw[:, 2, :]))
                link(V.tensor_scalar(a, ty, float(TRI), None, ALU.is_ge))
                link(V.tensor_scalar(b, ty, float(2 * TRI), None, ALU.is_ge))
                link(V.tensor_tensor(tg, a, b, ALU.add))
                link(V.scalar_tensor_tensor(rel3, tg, -float(TRI), ty, ALU.mult, ALU.add))
                for d in range(2):
                    node, other = raw[:, d, :], raw[:, 1 - d, :]
                    strip, loc, blk, pp = (ints[:, k, :] for k in range(4))
                    link(V.tensor_scalar(strip, node, STRIP.bit_length() - 1, None, ALU.logical_shift_right))
                    link(V.tensor_scalar(loc, node, STRIP - 1, None, ALU.bitwise_and))
                    link(V.tensor_scalar(blk, loc, NB - 1, None, ALU.bitwise_and))
                    link(V.tensor_scalar(pp, loc, NB.bit_length() - 1, None, ALU.logical_shift_right))
                    link(V.tensor_copy(stf, strip))
                    link(V.scalar_tensor_tensor(key[:, d, :], stf, float(NG), tg, ALU.mult, ALU.add))
                    link(V.tensor_scalar(pad, stf, float(NST), -float(FAR), ALU.is_ge, ALU.mult))
                    link(V.tensor_scalar(rec[:, d, :, 0], other, float(sh.N - 1), None, ALU.min))
                    link(V.scalar_tensor_tensor(a, blk, float(P), pp, ALU.mult, ALU.add))
                    link(V.tensor_tensor(rec[:, d, :, 1], a, pad, ALU.add))
                    link(V.scalar_tensor_tensor(a, blk, float(KK), pad, ALU.mult, ALU.add))
                    link(V.scalar_tensor_tensor(b, ty, 2.0, a, ALU.mult, ALU.add))
                    link(V.tensor_scalar(rec[:, d, :, 2], b, float(d), None, ALU.add))
                    link(V.tensor_copy(rec[:, d, :, 3], rel3))

                with v.Fori(0, GROUPS) as i:
                    for d in range(2):
                        v.wait_ge(hist_done, i * 2 + (d + 1))
                        for c in range(GRP):
                            ins = V.tensor_scalar(onehot[:, d, 0, c, :], iota[:, 0:DB + 1],
                                                  col(key[:, d, :], i * GRP + c), None, ALU.is_equal)
                        ins.then_inc(hot_ready, 1)
                v.wait_ge(hist_done, 2 * GROUPS + 3)
                for d in range(2):
                    link(V.tensor_scalar(cnti[:, :, d, :], ps_cnt[d][:, 0:DB].rearrange("p (s g) -> p s g", g=NG),
                                         float(P - 1), None, ALU.add))
                flat = "p s d g -> p (s d g)"
                ci = cnti[:, :, :, :].rearrange(flat)
                tl = tiles[:, :, :, :].rearrange(flat)
                link(V.tensor_scalar(ci, ci, 7, None, ALU.logical_shift_right))
                link(V.tensor_scalar(tl, ci, 1.0, None, ALU.max))
                link(V.tensor_tensor_scan(incl[:, :], onesrow[:, :], tl, 0.0, ALU.mult, ALU.add))
                NBIN = sh.BINS
                link(V.tensor_tensor(ts[:, 0:NBIN], incl[:, :], tl, ALU.subtract))
                link(V.tensor_copy(ts[:, NBIN:NBIN + 1], incl[:, NBIN - 1:NBIN]))
                ts6 = ts[:, 0:NBIN].rearrange("p (s d g) -> p s d g", d=2, g=NG)
                for d in range(2):
                    link(V.tensor_scalar(start[:, d, 0:DB].rearrange("p (s g) -> p s g", g=NG), ts6[:, :, d, :],
                                         0.0, None, ALU.add))
                    link(V.tensor_scalar(start[:, d, DB:DB + 1], ts[:, NBIN:NBIN + 1], float(d), None, ALU.add))
                v.sem_inc(base_ready, 1)
                def rounded(out_i, total):
                    link(V.tensor_scalar(toti[:, 0:1], total, float(UNROLL - 1), None, ALU.add))
                    link(V.tensor_scalar(toti[:, 1:2], toti[:, 0:1], 4, None, ALU.logical_shift_right))
                    link(V.tensor_scalar(out_i, toti[:, 1:2], float(UNROLL), None, ALU.mult))
                link(V.tensor_reduce(gcnt[:, :], tiles[:, :, 1, :], AX.X, ALU.add))
                link(V.tensor_tensor_scan(gincl[:, :], onesrow[:, 0:NST], gcnt[:, :], 0.0, ALU.mult, ALU.add))
                link(V.tensor_tensor(gs[:, 0:NST], gincl[:, :], gcnt[:, :], ALU.subtract))
                bounds = res["bounds"]
                link(V.tensor_copy(bounds[:, 0, 0:NST], ts6[:, :, 0, 0]))
                rounded(bounds[:, 0, NST:NST + 1], ts[:, NBIN:NBIN + 1])
                link(V.tensor_copy(bounds[:, 1, 0:NST], gs[:, 0:NST]))
                rounded(bounds[:, 1, NST:NST + 1], gincl[:, NST - 1:NST])
                link(V.tensor_copy(bounds[:, 2, 0:NST], ts6[:, :, 1, 0]))
                link(V.tensor_copy(bounds[:, 3, 0:NST], gcnt[:, :]))
                link(V.memset(pt[:, :, :], 0.0))
                for c in range(NTC):
                    me = tno[:, c:c + 1]
                    link(V.scalar_tensor_tensor(junk[:, :], ts[:, 0:NBIN], me, wmod[:, :], ALU.is_le, ALU.mult,
                                                accum_out=pt[:, 0, c:c + 1]))
                    link(V.scalar_tensor_tensor(junk[:, 0:NST], ts6[:, :, 0, 0], me, onesrow[:, 0:NST], ALU.is_le,
                                                ALU.mult, accum_out=pt[:, 1, c:c + 1]))
                    link(V.scalar_tensor_tensor(junk[:, 0:NST], ts6[:, :, 0, 0], me, onesrow[:, 0:NST], ALU.is_equal,
                                                ALU.mult, accum_out=pt[:, 2, c:c + 1]))
                for c in range(NGC):
                    me = tno[:, c:c + 1]
                    link(V.scalar_tensor_tensor(junk[:, 0:NST], gs[:, 0:NST], me, onesrow[:, 0:NST], ALU.is_le,
                                                ALU.mult, accum_out=pt[:, 3, c:c + 1]))
                    link(V.scalar_tensor_tensor(junk[:, 0:NST], gs[:, 0:NST], me, onesrow[:, 0:NST], ALU.is_equal,
                                                ALU.mult, accum_out=pt[:, 4, c:c + 1]))
                link(V.tensor_scalar(pti[:, 0, :], pt[:, 0, :], float(TRI * D), None, ALU.mult))
                for k in (1, 3):
                    link(V.tensor_scalar(pti[:, k, :], pt[:, k, :], -1.0, 0.0, ALU.add, ALU.max))
                link(V.tensor_copy(pti[:, 2, :], pt[:, 2, :]))
                V.tensor_copy(pti[:, 4, :], pt[:, 4, :]).then_inc(tiles_ready, 1)

                with v.Fori(0, GROUPS // 2) as i:
                    for h in range(2):
                        g = i * 2 + h
                        for d in range(2):
                            v.wait_ge(pos_ready[d], g * GRP + 1)
                            for c in range(GRP):
                                V.tensor_scalar(onehot[:, d, h, c, :], iota[:, 0:DB + 1],
                                                col(key[:, d, :], g * GRP + c), None, ALU.is_equal) \
                                    .then_inc(hot2_ready[d], 1)
                        for c in range(GRP):
                            for d in range(2):
                                v.wait_ge(pos_ready[d], g * GRP + (c + 2))
                                was, now = (h * GRP + c) % 2, (h * GRP + c + 1) % 2
                                V.tensor_tensor(sums[:, d, now, :], sums[:, d, was, :], onehot[:, d, h, c, :], ALU.add) \
                                    .then_inc(sums_ready[d], 1)
                                V.scalar_tensor_tensor(junk2[:, d, was, :], iota[:, 0:DB + 1],
                                                       col(key[:, d, :], g * GRP + c), ps_pos[d][:, was, 0:DB + 1],
                                                       ALU.is_equal, ALU.mult,
                                                       accum_out=posf[:, h, d, c:c + 1]).then_inc(pos_read[d], 1)
                        for d in range(2):
                            v.wait_ge(pos_read[d], g * GRP + (GRP + 2))
                        v.wait_ge(stage_free, g + 1)
                        k = g * 5
                        V.tensor_copy(posi[:, h, 0, :], posf[:, h, :, :].rearrange("p d c -> p (d c)")).then_inc(chain2, 1)
                        v.wait_ge(chain2, k + 1)
                        V.tensor_scalar(posi[:, h, 1, :], posi[:, h, 0, :], P - 1, None, ALU.bitwise_and).then_inc(chain2, 1)
                        V.tensor_scalar(posi[:, h, 2, :], posi[:, h, 0, :], 7, None, ALU.logical_shift_right).then_inc(chain2, 1)
                        v.wait_ge(chain2, k + 3)
                        V.scalar_tensor_tensor(rows[:, h, :], posi[:, h, 1, :], float(NT), posi[:, h, 2, :],
                                               ALU.mult, ALU.add).then_inc(chain2, 1)
                        for d in range(2):
                            ins = V.tensor_copy(recs[:, h, d * GRP:d * GRP + GRP, :],
                                                rec[:, d, bass.ds(g * GRP, GRP), :])
                        ins.then_inc(chain2, 1)
                        v.wait_ge(chain2, k + 5)
                        v.sem_inc(staged, 1)

            @block.scalar
            def _(act):
                act.sem_inc(hist_done, 2)
                for d in range(2):
                    act.sem_inc(pos_ready[d], 1)
                    act.sem_inc(pos_read[d], 2)
                    act.sem_inc(sums_ready[d], 1)
                act.sem_inc(stage_free, 2)

            @block.tensor
            def _(pe):
                pe.wait_ge(consts, 8)
                T = nc.tensor
                pe.wait_ge(hot_ready, 1)
                for d in range(2):
                    T.matmul(ps_cnt[d][:, 0:DB + 1], zero[:, 0:P], zero[:, 0:DB + 1], start=True, stop=False)
                with pe.Fori(0, GROUPS) as i:
                    for d in range(2):
                        pe.wait_ge(hot_ready, i * 2 + (d + 1))
                        for c in range(GRP):
                            ins = T.matmul(ps_cnt[d][:, 0:DB + 1], ones[:, :], onehot[:, d, 0, c, :],
                                           start=False, stop=False)
                        ins.then_inc(hist_done, 1)
                for d in range(2):
                    ins = T.matmul(ps_cnt[d][:, 0:DB + 1], zero[:, 0:P], zero[:, 0:DB + 1], start=False, stop=True)
                ins.then_inc(hist_done, 1)
                pe.wait_ge(base_ready, 1)
                with pe.Fori(0, GROUPS // 2) as i:
                    for h in range(2):
                        g = i * 2 + h
                        for c in range(GRP):
                            for d in range(2):
                                out = ps_pos[d][:, (h * GRP + c) % 2, 0:DB + 1]
                                pe.wait_ge(pos_read[d], g * GRP + (c + 1))
                                T.matmul(out, row0[:, :], start[:, d, :], start=True, stop=False)
                                pe.wait_ge(hot2_ready[d], g * GRP + (c + 1))
                                T.matmul(out, before[:, :], onehot[:, d, h, c, :], start=False, stop=False)
                                pe.wait_ge(sums_ready[d], g * GRP + (c + 1))
                                T.matmul(out, ones[:, :], sums[:, d, (h * GRP + c) % 2, :],
                                         start=False, stop=True).then_inc(pos_ready[d], 1)
        clear(nc, sems)


def build_coefs(nc, sh, dram, res):
    NST, NT = sh.NST, sh.NT
    NBLK = NST * NB
    W = NB * KK
    QUAD = 4
    tab, iota, ident = res["tab"], res["iota"], res["ident"]
    colf, coef3, bounds, bytile = res["colf"], res["coef3"], res["bounds"], res["bytile"]
    cself = res["cself"][:, 0:NBLK]
    sdeg, dinv = res["sdeg_s"][:, 2 * NB:2 * NB + NBLK], res["dinv_s"][:, 2 * NB:2 * NB + NBLK]
    gidx, gcol = res["gidx"], res["gcol"]

    sems = []
    with ExitStack() as ctx:
        def t(name, shape, dt=FP32):
            return ctx.enter_context(nc.sbuf_tensor("c_" + name, shape, dt))

        def sem(name):
            sems.append(ctx.enter_context(nc.semaphore("c_" + name)))
            return sems[-1]

        loc = t("loc", [P, NT], I32)
        locf = t("locf", [P, NT])
        place = t("place", [P, NT])
        rel3 = t("rel3", [P, NT])
        coef = t("coef", [P, NT])
        zero = t("zero", [P, P], BF16)
        identb = t("identb", [P, P], BF16)
        hot_p = t("hot_p", [P, 2, QUAD, P], BF16)
        hot_w = t("hot_w", [P, 2, QUAD, W], BF16)
        hot_t = t("hot_t", [P, 2, QUAD, P])
        cnt = t("cnt", [P, NBLK, KK])
        pa = t("pa", [P, NBLK, KK])
        pb = t("pb", [P, NBLK, KK])
        stage = t("stage", [P, 2, NB, KK + 1])
        cbt = t("cbt", [KK + 1, 2, STRIP])
        junk = t("junk", [P, 2, QUAD, W])
        ps_cnt = ctx.enter_context(nc.psum_tensor("c_ps_cnt", [P, 2, 512], FP32))
        ps_t = ctx.enter_context(nc.psum_tensor("c_ps_t", [P, 2, 1024], BF16))
        ps_q = ctx.enter_context(nc.psum_tensor("c_ps_q", [P, 2, 512], FP32))

        chain, hot_ready, cnt_mm, cnt_out = sem("chain"), sem("hot_ready"), sem("cnt_mm"), sem("cnt_out")
        coefs_ready, staged, cb_ps, cb_sb = sem("coefs_ready"), sem("staged"), sem("cb_ps"), sem("cb_sb")
        closed = sem("closed")
        cb_free, cb_out = sem("cb_free"), [sem("cb_out0"), sem("cb_out1")]
        hp_ready, hp_ps, hp_sb = sem("hp_ready"), sem("hp_ps"), sem("hp_sb")
        q_ps, q_read = sem("q_ps"), sem("q_read")
        col_ready, glist = sem("col_ready"), sem("glist")

        def total(eng):
            return eng.value_load(bounds[0:1, 0, NST:NST + 1], min_val=UNROLL, max_val=NT - UNROLL)

        with nc.Block() as block:
            @block.vector
            def _(v):
                n = [0]
                V = nc.vector

                def link(ins):
                    n[0] += 1
                    ins.then_inc(chain, 1)
                    v.wait_ge(chain, n[0])

                V.memset(gcol[:, :], -1.0)
                V.memset(res["cself"][:, :], 0.0)
                V.memset(res["sdeg_s"][:, :], 1.0)
                V.memset(res["dinv_s"][:, :], 1.0)
                link(V.memset(gidx[:, :], 0))
                V.memset(zero[:, :], 0.0)
                V.tensor_copy(identb[:, :], ident[:, :])
                link(V.tensor_copy(colf[:, :], tab[:, :, 1]))
                v.sem_inc(col_ready, 1)
                V.tensor_copy(place[:, :], tab[:, :, 2])
                V.tensor_copy(rel3[:, :], tab[:, :, 3])
                link(V.memset(coef[:, :], 0.0))
                link(V.tensor_scalar(loc[:, :], tab[:, :, 1], P - 1, None, ALU.bitwise_and))
                link(V.tensor_copy(locf[:, :], loc[:, :]))
                T = total(v)
                with v.Fori(0, T, 2 * QUAD) as t0:
                    for h in range(2):
                        v.wait_ge(cnt_mm, t0 + (h + 1) * QUAD)
                        for k in range(QUAD):
                            V.tensor_scalar(hot_p[:, h, k, :], iota[:, 0:P], col(locf, t0 + (h * QUAD + k)), None,
                                            ALU.is_equal)
                            V.tensor_scalar(hot_w[:, h, k, :], iota[:, 0:W], col(place, t0 + (h * QUAD + k)), None,
                                            ALU.is_equal).then_inc(hot_ready, 1)
                v.wait_ge(cnt_out, NST + 2)
                link(V.tensor_scalar(pa[:, :, :], cnt[:, :, :], 1.0, None, ALU.max))
                link(V.reciprocal(pb[:, :, :], pa[:, :, :]))
                link(V.tensor_scalar(pa[:, :, :], pb[:, :, :], 2.0, None, ALU.mult))
                a, b = pa, pb
                s = 1
                while s < KK:
                    V.tensor_tensor(b[:, :, 0:KK - s], a[:, :, 0:KK - s], a[:, :, s:KK], ALU.mult)
                    link(V.tensor_copy(b[:, :, KK - s:KK], a[:, :, KK - s:KK]))
                    a, b = b, a
                    s *= 2
                assert a is pb
                link(V.tensor_copy(cself[:, :], pb[:, :, 0]))
                link(V.tensor_reduce(dinv[:, :], cnt[:, :, :].rearrange("p b (r d) -> p b d r", d=2)[:, :, 1, :],
                                     AX.X, ALU.add))
                link(V.tensor_scalar(sdeg[:, :], dinv[:, :], 1.0, None, ALU.add))
                v.sem_inc(coefs_ready, 1)
                v.wait_ge(coefs_ready, 2)
                link(V.reciprocal(dinv[:, :], sdeg[:, :]))
                link(V.tensor_tensor(pa[:, :, :], cnt[:, :, :], pb[:, :, :], ALU.mult))
                with v.Fori(0, NST // 2) as pair:
                    j = pair * 2
                    for h in range(2):
                        v.wait_ge(cb_ps, j + (h + 1))
                        b0 = (j + h) * NB
                        V.tensor_copy(stage[:, h, :, 0:KK], pa[:, bass.ds(b0, NB), :])
                        V.tensor_copy(stage[:, h, :, KK:KK + 1], pb[:, bass.ds(b0, NB), 0:1]).then_inc(staged, 1)

                def hots(t0, h):
                    v.wait_ge(hp_ps, t0 + QUAD)
                    for k in range(QUAD):
                        V.tensor_scalar(hot_p[:, h, k, :], iota[:, 0:P], col(locf, t0 + k), None,
                                        ALU.is_equal).then_inc(hp_ready, 1)

                v.wait_ge(hp_ps, QUAD)
                for k in range(QUAD):
                    V.tensor_scalar(hot_p[:, 0, k, :], iota[:, 0:P], locf[:, k:k + 1], None,
                                    ALU.is_equal).then_inc(hp_ready, 1)
                with v.Fori(0, T, 2 * QUAD) as t0:
                    for h in range(2):
                        hots(t0 + (h + 1) * QUAD, 1 - h)
                        v.wait_ge(q_ps, t0 + (h + 1) * QUAD)
                        for k in range(QUAD):
                            V.scalar_tensor_tensor(junk[:, h, k, :], iota[:, 0:W], col(place, t0 + (h * QUAD + k)),
                                                   ps_q[:, h, k * W:k * W + W], ALU.is_equal, ALU.mult,
                                                   accum_out=col(coef, t0 + (h * QUAD + k))).then_inc(q_read, 1)
                v.wait_ge(q_read, T + 2 * QUAD)
                for i in range(TRI):
                    V.scalar_tensor_tensor(coef3[:, :, i], rel3[:, :], float(i), coef[:, :], ALU.is_equal, ALU.mult)

            @block.gpsimd
            def _(pool):
                pool.wait_ge(col_ready, 1)
                with pool.Fori(0, NST) as j:
                    u0 = pool.value_load(bounds[0:1, 1, bass.ds(j, 1)], min_val=0, max_val=sh.NTG - 1)
                    t0 = pool.value_load(bounds[0:1, 2, bass.ds(j, 1)], min_val=0, max_val=NT - 1)
                    m = pool.value_load(bounds[0:1, 3, bass.ds(j, 1)], min_val=1, max_val=NT - 1)
                    with pool.Fori(0, m) as i:
                        at = within(u0 + i, sh.NTG - 1)
                        of = within(t0 + i, NT - 1)
                        nc.gpsimd.tensor_copy(gidx[:, bass.ds(at, 1)], tab[:, bass.ds(of, 1), 0])
                        nc.gpsimd.tensor_copy(gcol[:, bass.ds(at, 1)], colf[:, bass.ds(of, 1)])

            @block.sync
            def _(sp):
                with sp.Fori(0, NST // 2) as pair:
                    j = pair * 2
                    for h in range(2):
                        sp.wait_ge(cb_sb, j + (h + 1))
                        sp.dma_start(dram["cbt"][bass.ds(j + h, 1), :, :].rearrange("s k n -> (s k) n"),
                                     cbt[:, h, :]).then_inc(cb_out[h], 16)
                        sp.wait_ge(cb_out[h], j * 8 + 16)
                        sp.sem_inc(cb_free, 1)

            @block.scalar
            def _(act):
                act.sem_inc(cnt_mm, 2 * QUAD)
                act.sem_inc(cnt_out, 2)
                act.sem_inc(cb_ps, 1)
                act.sem_inc(cb_free, 2)
                act.sem_inc(hp_ps, 2 * QUAD)
                act.sem_inc(hp_sb, 2 * QUAD)
                act.sem_inc(q_read, 2 * QUAD)
                C = nc.scalar
                with act.Fori(0, NST) as j:
                    act.wait_ge(closed, j + 2)
                    C.activation(cnt[:, bass.ds(j * NB, NB), :].rearrange("p b k -> p (b k)"),
                                 ps_cnt[:, bass.ds(j % 2, 1), 0:W].rearrange("p o w -> p (o w)"),
                                 ACT.Copy).then_inc(cnt_out, 1)
                act.wait_ge(coefs_ready, 1)
                C.activation(sdeg[:, :], sdeg[:, :], ACT.Sqrt).then_inc(coefs_ready, 1)
                with act.Fori(0, NST // 2) as pair:
                    j = pair * 2
                    for h in range(2):
                        act.wait_ge(cb_ps, j + (h + 2))
                        act.wait_ge(cb_free, j + (h + 1))
                        C.activation(cbt[:, h, :], ps_cnt[0:KK + 1, h, :], ACT.Copy).then_inc(cb_sb, 1)

                def turn(q1, h):
                    act.wait_ge(hp_ps, q1 + 3 * QUAD)
                    C.activation(hot_t[:, h, :, :].rearrange("p k m -> p (k m)"), ps_t[:, h, 0:QUAD * P],
                                 ACT.Copy).then_inc(hp_sb, QUAD)

                act.wait_ge(hp_ps, 3 * QUAD)
                C.activation(hot_t[:, 0, :, :].rearrange("p k m -> p (k m)"), ps_t[:, 0, 0:QUAD * P],
                             ACT.Copy).then_inc(hp_sb, QUAD)
                T = total(act)
                with act.Fori(0, T, 2 * QUAD) as t0:
                    for h in range(2):
                        turn(t0 + (h + 1) * QUAD, 1 - h)

            @block.tensor
            def _(pe):
                M = nc.tensor
                T = total(pe)

                def bank(j):
                    return ps_cnt[:, bass.ds(j % 2, 1), 0:W].rearrange("p o w -> p (o w)")

                pe.wait_ge(hot_ready, 1)
                M.matmul(bank(1), zero[:, :], hot_w[:, 0, 0, :], start=True, stop=False)
                with pe.Fori(0, T, 2 * QUAD) as t0:
                    for h in range(2):
                        for k in range(QUAD):
                            tt = t0 + (h * QUAD + k)
                            j = pe.value_load(bytile[0:1, bass.ds(tt + NT, 1)], min_val=0, max_val=NST - 1)
                            first = pe.value_load(bytile[0:1, bass.ds(tt + 2 * NT, 1)], min_val=0, max_val=1)
                            pe.wait_ge(hot_ready, tt + 1)
                            with pe.If(first):
                                M.matmul(bank(j + 1), zero[:, :], hot_w[:, h, k, :], start=False, stop=True).then_inc(closed, 1)
                                pe.wait_ge(cnt_out, j + 1)
                                M.matmul(bank(j), zero[:, :], hot_w[:, h, k, :], start=True, stop=False)
                            M.matmul(bank(j), hot_p[:, h, k, :], hot_w[:, h, k, :], start=False, stop=False).then_inc(cnt_mm, 1)
                M.matmul(bank(NST - 1), zero[:, :], hot_w[:, 0, 0, :], start=False, stop=True).then_inc(closed, 1)
                with pe.Fori(0, NST // 2) as pair:
                    j = pair * 2
                    for h in range(2):
                        pe.wait_ge(staged, j + (h + 1))
                        pe.wait_ge(cb_free, j + (h + 1))
                        for b in range(NB):
                            ins = M.transpose(ps_cnt[0:KK + 1, h, b * P:b * P + P], stage[:, h, b, :], ident[:, :])
                        ins.then_inc(cb_ps, 1)

                def turn(q1, h):
                    pe.wait_ge(hp_ready, q1 + QUAD)
                    for k in range(QUAD):
                        M.transpose(ps_t[:, h, k * P:k * P + P], hot_p[:, h, k, :], identb[:, :]).then_inc(hp_ps, 1)

                pe.wait_ge(hp_ready, QUAD)
                for k in range(QUAD):
                    M.transpose(ps_t[:, 0, k * P:k * P + P], hot_p[:, 0, k, :], identb[:, :]).then_inc(hp_ps, 1)
                with pe.Fori(0, T, 2 * QUAD) as t0:
                    for h in range(2):
                        pe.wait_ge(hp_sb, t0 + (h + 2) * QUAD)
                        turn(t0 + (h + 1) * QUAD, 1 - h)
                        pe.wait_ge(hp_sb, t0 + (h + 3) * QUAD)
                        pe.wait_ge(q_read, t0 + (h + 1) * QUAD)
                        for k in range(QUAD):
                            tt = t0 + (h * QUAD + k)
                            j = pe.value_load(bytile[0:1, bass.ds(tt + NT, 1)], min_val=0, max_val=NST - 1)
                            M.matmul(ps_q[:, h, k * W:k * W + W], hot_t[:, h, k, :],
                                     pb[:, bass.ds(j * NB, NB), :].rearrange("p b k -> p (b k)"),
                                     start=True, stop=True).then_inc(q_ps, 1)
        clear(nc, sems)


def layer(nc, sh, name, rgcn, last, gathered, own, residual, to, weights, bias, dram, res):
    NST, NT = sh.NST, sh.NT
    iota, ident = res["iota"], res["ident"]
    bounds, bytile = res["bounds"], res["bytile"]
    which = 0 if rgcn else 1
    col_of = res["colf"] if rgcn else res["gcol"]
    strip_row, first_row = (1, 2) if rgcn else (3, 4)
    bound_max = NT if rgcn else sh.NTG
    least = 2 * NG if rgcn else NG
    cself, coef3 = res["cself"], res["coef3"]
    LAND = 4
    AHEAD = 6

    sems = []
    with ExitStack() as ctx:
        def t(n_, shape, dt=FP32):
            return ctx.enter_context(nc.sbuf_tensor(f"{name}_{n_}", shape, dt))

        def ps(n_, shape):
            return ctx.enter_context(nc.psum_tensor(f"{name}_{n_}", shape, FP32))

        def sem(n_):
            sems.append(ctx.enter_context(nc.semaphore(f"{name}_{n_}")))
            return sems[-1]

        xg = t("xg", [P, RING, D])
        gi = t("gi", [P, 2, RING], I32)
        xin = t("xin", [P, 2, STRIP])
        xres = t("xres", [P, 2, STRIP])
        xc = t("xc", [P, STRIP])
        xt = t("xt", [D, STRIP])
        ht = t("ht", [D, STRIP])
        sel = t("sel", [P, 2, STRIP])
        outb = t("outb", [P, 2, STRIP])
        eps = t("eps", [P, 1])
        zero = t("zero", [P, STRIP], BF16)
        if rgcn:
            wall = t("wall", [D, KK * D])
            wself = t("wself", [D, D])
            ball = t("ball", [KK + 1, D])
            cb = t("cb", [KK + 1, 2, STRIP])
            turned = t("turned", [P, 2, P])
            part = t("part", [P, 2, D])
            y = t("y", [P, 2, D])
            ps_xt = ps("ps_xt", [P, 2, 512])
            ps_y = ps("ps_y", [P, 2, 512])
        else:
            wgcn = t("wgcn", [D, D])
            brow = t("brow", [P, D])
        if last:
            z = t("z", [P, STRIP])
            stats = t("stats", [P, NB, 6])
            mv = t("mv", [P, NB, 2])
            sd = t("sd", [P, NB])
            rs = t("rs", [P, NB])
            rs2 = t("rs2", [P, NB])
        if not rgcn:
            za = t("za", [P, STRIP])
            zb = t("zb", [P, STRIP])
        ps_h = ps("ps_h", [P, 2, STRIP])
        ps_x = ps("ps_x", [P, STRIP])
        ps_o = ps("ps_o", [P, STRIP])

        landed = res["landed"][name]
        w_in, consts, gate, idx_ready = sem("w_in"), sem("consts"), sem("gate"), sem("idx_ready")
        rows_in = sem("rows_in")
        xt_ps, xt_sb = sem("xt_ps"), sem("xt_sb")
        y_ps, y_part, y_sb = sem("y_ps"), sem("y_part"), sem("y_sb")
        sel_sb, tile_done = sem("sel_sb"), sem("tile_done")
        rows_used = xt_ps if rgcn else tile_done
        in_land, in_ready, in_free = [sem("in_land0"), sem("in_land1")], sem("in_ready"), sem("in_free")
        cb_land, cb_ready, closed = [sem("cb_land0"), sem("cb_land1")], sem("cb_ready"), sem("closed")
        res_land, res_ready = [sem("res_land0"), sem("res_land1")], sem("res_ready")
        xc_sb, own_ps, own_sb = sem("xc_sb"), sem("own_ps"), sem("own_sb")
        ht_sb, out_ps, fin = sem("ht_sb"), sem("out_ps"), sem("fin")
        passed = sem("passed")
        fin_chain, var_ready, sd_ready = sem("fin_chain"), sem("var_ready"), sem("sd_ready")
        st_land, out_free = [sem("st_land0"), sem("st_land1")], sem("out_free")

        def strip_rows(a, j, n_rows=STRIP):
            start = j * STRIP
            rows = a[start:start + n_rows, :] if isinstance(j, int) else a[bass.ds(start, n_rows), :]
            return rows.rearrange("(p b) d -> p (b d)", b=NB)

        def total(eng):
            return eng.value_load(bounds[0:1, which, NST:NST + 1], min_val=UNROLL, max_val=bound_max - UNROLL)

        def tiles_of(eng, j):
            lo = eng.value_load(bounds[0:1, which, bass.ds(j, 1)], min_val=0, max_val=bound_max - UNROLL)
            hi = eng.value_load(bounds[0:1, which, bass.ds(j + 1, 1)], min_val=least, max_val=bound_max)
            return lo, hi

        def half(tens, i):
            return tens[:, bass.ds(i % 2, 1), :].rearrange("p o n -> p (o n)")

        with nc.Block() as block:
            @block.gpsimd
            def _(pool):
                idx = res["tab"] if rgcn else res["gidx"]
                T = total(pool)
                with pool.Fori(0, T, UNROLL) as t0:
                    src_ap = idx[:, bass.ds(t0, UNROLL), 0] if rgcn else idx[:, bass.ds(t0, UNROLL)]
                    nc.gpsimd.tensor_copy(gi[:, :, :].rearrange("p a b -> p (a b)"), src_ap).then_inc(idx_ready, UNROLL)
                    pool.wait_ge(idx_ready, t0 + UNROLL)
                    pool.sem_inc(gate, 1)
                    for k in range(UNROLL + LAND):
                        if k < UNROLL:
                            pool.wait_ge(rows_used, t0 + (k + 1))
                            pool.sem_inc(gate, 1)
                            nc.gpsimd.indirect_dma_start(
                                xg[:, k % RING, :], None, gathered[0:sh.N, :],
                                bass.IndirectOffsetOnAxis(ap=gi[:, k // RING, k % RING:k % RING + 1], axis=0)) \
                                .then_inc(landed[k % RING], 16)
                        if k >= LAND:
                            m = k - LAND
                            pool.wait_ge(landed[m % RING], t0 * (16 // RING) + 16 * (m // RING + 1))
                            pool.sem_inc(rows_in, 1)
                if rgcn:
                    nc.gpsimd.tensor_copy(gi[:, 0, 0:2], idx[:, bass.ds(T, 2), 0]).then_inc(idx_ready, 1)
                    pool.wait_ge(idx_ready, T + 1)
                    pool.sem_inc(gate, 1)
                    for k in range(2):
                        pool.wait_ge(rows_used, T + (k + 1))
                        pool.sem_inc(gate, 1)
                        nc.gpsimd.indirect_dma_start(
                            xg[:, k, :], None, gathered[0:sh.N, :],
                            bass.IndirectOffsetOnAxis(ap=gi[:, 0, k:k + 1], axis=0)).then_inc(landed[k], 16)
                    for k in range(2):
                        pool.wait_ge(landed[k], T * (16 // RING) + 16)
                        pool.sem_inc(rows_in, 1)

            @block.sync
            def _(sp):
                if rgcn:
                    for d in range(2):
                        sp.dma_start(wall[:, d * R * D:(d + 1) * R * D].rearrange("k (r m) -> k r m", m=D),
                                     weights[d * R:(d + 1) * R, :, :].rearrange("r k m -> k r m")).then_inc(w_in, 16)
                        sp.dma_start(ball[d:KK:2, :], bias[d * R:(d + 1) * R, :]).then_inc(w_in, 16)
                    sp.dma_start(wself[:, :], weights[KK, :, :]).then_inc(w_in, 16)
                    sp.dma_start(ball[KK:KK + 1, :], bias[KK:KK + 1, :]).then_inc(w_in, 16)
                else:
                    sp.dma_start(wgcn[:, :], weights).then_inc(w_in, 16)
                    sp.dma_start(brow[:, :], bias.rearrange("(o d) -> o d", o=1).to_broadcast([P, D])).then_inc(w_in, 16)

                def step(j, h):
                    fixed = isinstance(j, int)
                    if not fixed or j <= NST:
                        sp.wait_ge(in_free, j + 1)
                        jj = j if not fixed or j < NST else 0
                        if fixed and j == NST - 1:
                            sp.dma_start(xin[0:sh.LAST // NB, h, :], strip_rows(own, j, sh.LAST)).then_inc(in_land[h], 16)
                        else:
                            sp.dma_start(xin[:, h, :], strip_rows(own, jj)).then_inc(in_land[h], 16)
                    if not fixed or 1 <= j <= NST + 1:
                        sp.wait_ge(in_land[1 - h], (j - 1 - (1 - h)) * 8 + 16)
                        sp.sem_inc(in_ready, 1)
                    if rgcn and (not fixed or 1 <= j <= NST):
                        sp.wait_ge(closed, j)
                        sp.dma_start(cb[:, 1 - h, :], dram["cbt"][bass.ds(j - 1, 1), :, :].rearrange("s k n -> (s k) n")) \
                            .then_inc(cb_land[1 - h], 16)
                    if rgcn and (not fixed or 2 <= j <= NST + 1):
                        sp.wait_ge(cb_land[h], (j - 2 - h) * 8 + 16)
                        sp.sem_inc(cb_ready, 1)
                    if last and (not fixed or 3 <= j < NST + 3):
                        sp.wait_ge(fin, j - 1)
                        k = j - 3
                        if fixed and k == NST - 1:
                            sp.dma_start(xres[0:sh.LAST // NB, 1 - h, :], strip_rows(residual, k, sh.LAST)).then_inc(res_land[1 - h], 16)
                        else:
                            sp.dma_start(xres[:, 1 - h, :], strip_rows(residual, k)).then_inc(res_land[1 - h], 16)
                    if last and (not fixed or 4 <= j < NST + 4):
                        sp.wait_ge(res_land[h], (j - 4 - h) * 8 + 16)
                        sp.sem_inc(res_ready, 1)
                    if not fixed or 5 <= j < NST + 5:
                        k = j - 5
                        sp.wait_ge(fin, k + 4)
                        if fixed and k == NST - 1:
                            sp.dma_start(strip_rows(to, k, sh.LAST), outb[0:sh.LAST // NB, 1 - h, :]).then_inc(st_land[1 - h], 16)
                        else:
                            sp.dma_start(strip_rows(to, k), outb[:, 1 - h, :]).then_inc(st_land[1 - h], 16)
                    if not fixed or 6 <= j < NST + 6:
                        sp.wait_ge(st_land[h], (j - 6 - h) * 8 + 16)
                        sp.sem_inc(out_free, 1)

                for j in range(AHEAD):
                    step(j, j % 2)
                with sp.Fori(AHEAD // 2, (NST - 2) // 2) as pair:
                    for h in range(2):
                        step(pair * 2 + h, h)
                for j in range(NST - 2, NST + AHEAD):
                    step(j, j % 2)

            @block.vector
            def _(v):
                V = nc.vector
                V.memset(ps_h[:, 1, :], 0.0).then_inc(consts, 1)
                V.memset(ht[:, :], 0.0).then_inc(consts, 1)
                V.memset(outb[:, :, :], 0.0).then_inc(consts, 1)
                V.memset(xin[:, :, :], 0.0).then_inc(consts, 1)
                V.memset(eps[:, :], EPS).then_inc(consts, 1)
                V.memset(xres[:, :, :], 0.0).then_inc(consts, 1)
                V.memset(xt[:, :], 0.0).then_inc(consts, 1)
                V.memset(cb[:, 1, :] if rgcn else sel[:, 1, :], 0.0).then_inc(consts, 1)
                V.memset(zero[:, :], 0.0).then_inc(consts, 1)
                v.wait_ge(consts, 9)
                v.sem_inc(in_free, 2)
                v.sem_inc(res_ready, 2)
                v.sem_inc(out_free, 4)
                v.sem_inc(tile_done, RING)
                if rgcn:
                    v.sem_inc(xt_ps, RING)
                v.sem_inc(closed, 1)
                v.sem_inc(own_sb, 1)
                if rgcn:
                    v.sem_inc(cb_ready, 1)
                v.wait_ge(w_in, 96 if rgcn else 32)

                def own_rows(j):
                    v.wait_ge(in_ready, j + 1)
                    if not isinstance(j, int) or j >= 1:
                        v.wait_ge(own_ps, j)
                    if rgcn:
                        out = xc[:, :].rearrange("p (b d) -> p b d", b=NB)
                        c = cself[:, bass.ds(j * NB, NB)].unsqueeze(2).to_broadcast([P, NB, D])
                        V.tensor_tensor(out, half(xin, j).rearrange("p (b d) -> p b d", b=NB), c, ALU.mult).then_inc(xc_sb, 1)
                    else:
                        V.tensor_copy(xc[:, :], half(xin, j)).then_inc(xc_sb, 1)
                    v.wait_ge(xc_sb, j + 1)
                    v.sem_inc(in_free, 1)

                def message(tt):
                    v.wait_ge(tile_done, tt + (RING - 1))
                    s = V.tensor_scalar(half(sel, tt), iota[:, :], col(col_of, tt), None, ALU.is_equal)
                    s.then_inc(sel_sb, 1)
                    if not rgcn:
                        return
                    v.wait_ge(y_ps, tt + 1)
                    pa = half(part, tt)
                    prods = ps_y[:, bass.ds(tt % 2, 1), 0:TRI * D].rearrange("p o n -> p (o n)")
                    c = [coef3[:, bass.ds(tt, 1), i] for i in range(TRI)]
                    V.tensor_scalar(pa, prods[:, 0:D], c[0], None, ALU.mult).then_inc(y_part, 1)
                    v.wait_ge(y_part, tt * 2 + 1)
                    V.scalar_tensor_tensor(pa, prods[:, D:2 * D], c[1], pa, ALU.mult, ALU.add).then_inc(y_part, 1)
                    v.wait_ge(y_part, tt * 2 + 2)
                    V.scalar_tensor_tensor(half(y, tt), prods[:, 2 * D:3 * D], c[2], pa, ALU.mult, ALU.add).then_inc(y_sb, 1)

                def blocks(a):
                    return [a[:, b * D:b * D + D] for b in range(NB)]

                LINKS = {(True, False): 0, (True, True): 6, (False, False): 2, (False, True): 8}[(rgcn, last)]

                def finish(k):
                    v.wait_ge(out_ps, k + 3)
                    v.wait_ge(out_free, k + 3)
                    base = (k + 2) * LINKS
                    count = [0]
                    dst = half(outb, k + 2)
                    node0 = (k + 2) * NB

                    def link(ins):
                        count[0] += 1
                        ins.then_inc(fin_chain, 1)
                        v.wait_ge(fin_chain, base + count[0])

                    def scale(a):
                        return [a[:, bass.ds(node0 + b, 1)] for b in range(NB)]

                    if rgcn and not last:
                        V.tensor_scalar(dst, ps_o[:, :], 0.0, None, ALU.max).then_inc(fin, 1)
                        return
                    if not rgcn:
                        di = scale(res["dinv_s"])
                        for b in range(NB):
                            ins = V.scalar_tensor_tensor(blocks(za)[b], blocks(ps_o)[b], di[b], brow[:, :], ALU.mult, ALU.add)
                        link(ins)
                    if not rgcn and not last:
                        for b in range(NB):
                            ins = V.tensor_scalar(blocks(dst)[b], blocks(za)[b], 0.0, di[b], ALU.max, ALU.mult)
                        link(ins)
                        v.sem_inc(fin, 1)
                        return
                    v.wait_ge(res_ready, k + 3)
                    xr = half(xres, k + 2)
                    if rgcn:
                        link(V.tensor_tensor(z[:, :], ps_o[:, :], xr, ALU.add))
                    else:
                        link(V.tensor_scalar(zb[:, :], za[:, :], 0.0, None, ALU.max))
                        sq = scale(res["sdeg_s"])
                        for b in range(NB):
                            ins = V.scalar_tensor_tensor(blocks(z)[b], blocks(xr)[b], sq[b], blocks(zb)[b], ALU.mult, ALU.add)
                        link(ins)
                    for b in range(NB):
                        ins = V.bn_stats(stats[:, b, :], blocks(z)[b])
                    link(ins)
                    v.sem_inc(passed, 1)
                    for b in range(NB):
                        ins = V.bn_aggr(mv[:, b, :], stats[:, b, :])
                    link(ins)
                    v.sem_inc(var_ready, 1)
                    v.wait_ge(sd_ready, k + 3)
                    link(V.reciprocal(rs[:, :], sd[:, :]))
                    if rgcn:
                        di = res["dinv_s"][:, bass.ds(node0, NB)]
                        link(V.tensor_tensor(rs2[:, :], rs[:, :], di, ALU.mult))
                    else:
                        link(V.tensor_copy(rs2[:, :], rs[:, :]))
                    for b in range(NB):
                        ins = V.tensor_scalar(blocks(dst)[b], blocks(z)[b], mv[:, b, 0:1], rs2[:, b:b + 1],
                                              ALU.subtract, ALU.mult)
                    link(ins)
                    v.sem_inc(fin, 1)

                own_rows(0)
                with v.Fori(0, NST) as j:
                    lo, hi = tiles_of(v, j)
                    message(lo)
                    own_rows(j + 1)
                    message(lo + 1)
                    finish(j - 2)
                    with v.Fori(lo + 2, hi) as tt:
                        message(tt)
                finish(NST - 2)
                finish(NST - 1)

            @block.scalar
            def _(act):
                C = nc.scalar
                act.sem_inc(ht_sb, 1)
                act.sem_inc(fin, 1)
                act.wait_ge(consts, 9)

                def own_turned(j):
                    act.wait_ge(own_ps, j + 1)
                    C.activation(xt[:, :], ps_x[:, :], ACT.Copy).then_inc(own_sb, 1)

                def hidden(k):
                    act.wait_ge(out_ps, k + 2)
                    act.wait_ge(closed, k + 3)
                    C.activation(ht[:, :], half(ps_h, k + 2), ACT.Copy).then_inc(ht_sb, 1)

                def turned_copy(tt):
                    act.wait_ge(xt_ps, tt + (1 + RING))
                    C.activation(half(turned, tt), half(ps_xt, tt)[:, 0:P], ACT.Copy).then_inc(xt_sb, 1)

                def deviation(k):
                    act.wait_ge(var_ready, k + 3)
                    C.activation(sd[:, :], mv[:, :, 1], ACT.Sqrt, bias=eps[:, 0:1]).then_inc(sd_ready, 1)

                if rgcn:
                    turned_copy(0)
                    turned_copy(1)
                with act.Fori(0, NST) as j:
                    lo, hi = tiles_of(act, j)
                    own_turned(j)
                    hidden(j - 1)
                    if rgcn:
                        with act.Fori(lo, lo + 2) as tt:
                            turned_copy(tt + 2)
                    if last:
                        deviation(j - 2)
                    if rgcn:
                        with act.Fori(lo + 2, hi) as tt:
                            turned_copy(tt + 2)
                hidden(NST - 1)
                if last:
                    deviation(NST - 2)
                    deviation(NST - 1)

            @block.tensor
            def _(pe):
                M = nc.tensor
                T = total(pe)
                pe.wait_ge(w_in, 96 if rgcn else 32)
                pe.wait_ge(consts, 9)

                def turn_tile(tt, k):
                    pe.wait_ge(rows_in, tt + 1)
                    M.transpose(ps_xt[:, k % 2, 0:P], xg[:, k % RING, :], ident[:, :]).then_inc(xt_ps, 1)

                def product(tt, k):
                    pe.wait_ge(xt_sb, tt + 1)
                    off = pe.value_load(bytile[0:1, bass.ds(tt, 1)], min_val=0, max_val=(2 * NG - 1) * TRI * D)
                    M.matmul(ps_y[:, k % 2, 0:TRI * D], turned[:, k % 2, :], wall[:, bass.ds(off, TRI * D)],
                             start=True, stop=True).then_inc(y_ps, 1)

                def own_turn(j):
                    pe.wait_ge(xc_sb, j + 1)
                    for b in range(NB):
                        ins = M.transpose(ps_x[:, b * P:b * P + P], xc[:, b * D:b * D + D], ident[:, :])
                    ins.then_inc(own_ps, 1)

                def out(k):
                    pe.wait_ge(ht_sb, k + 3)
                    pe.wait_ge(fin, k + 3)
                    for b in range(NB):
                        dst, hb = ps_o[:, b * D:b * D + D], ht[:, b * P:b * P + P]
                        ins = M.transpose(dst, hb, ident[:, :]) if rgcn else M.matmul(dst, hb, wgcn[:, :], start=True, stop=True)
                    ins.then_inc(out_ps, 1)

                def close(k):
                    pe.wait_ge(own_sb, k + 2)
                    if rgcn:
                        pe.wait_ge(cb_ready, k + 2)
                        M.matmul(half(ps_h, k + 2), ball[:, :], half(cb, k + 2), start=False, stop=False)
                        M.matmul(half(ps_h, k + 2), wself[:, :], xt[:, :], start=False, stop=True).then_inc(closed, 1)
                    else:
                        M.matmul(half(ps_h, k + 2), ident[:, :], xt[:, :], start=False, stop=True).then_inc(closed, 1)

                M.matmul(ps_h[:, 1, :], zero[:, 0:P], zero[:, :], start=True, stop=False)
                if rgcn:
                    turn_tile(0, 0)
                    turn_tile(1, 1)
                    product(0, 0)
                with pe.Fori(0, T, RING) as t0:
                    for k in range(RING):
                        tt = t0 + k
                        if rgcn:
                            turn_tile(tt + 2, k + 2)
                            product(tt + 1, k + 1)
                        else:
                            pe.wait_ge(rows_in, tt + 1)
                        j = pe.value_load(bytile[0:1, bass.ds(tt + strip_row * NT, 1)], min_val=0, max_val=NST - 1)
                        first = pe.value_load(bytile[0:1, bass.ds(tt + first_row * NT, 1)], min_val=0, max_val=1)
                        acc = half(ps_h, j)
                        lhs = y[:, k % 2, :] if rgcn else xg[:, k, :]
                        made = y_sb if rgcn else sel_sb
                        with pe.If(first):
                            close(j - 1)
                            out(j - 2)
                            own_turn(j)
                            pe.wait_ge(made, tt + 1)
                            M.matmul(acc, lhs, half(sel, k), start=True, stop=False).then_inc(tile_done, 1)
                        with pe.Else():
                            pe.wait_ge(made, tt + 1)
                            M.matmul(acc, lhs, half(sel, k), start=False, stop=False).then_inc(tile_done, 1)
                close(NST - 1)
                out(NST - 2)
                out(NST - 1)
        clear(nc, sems)


def program(nc, x, src, dst, edge_type, w0, b0, w1, b1, w2, b2, out, dram):
    sh = Shapes(x.shape[0], src.shape[0])
    assert sh.NST % 2 == 0 and sh.N % NB == 0 and sh.NST >= 10
    NBLK = sh.NST * NB
    with ExitStack() as ctx:
        def t(name, shape, dt=FP32):
            return ctx.enter_context(nc.sbuf_tensor(name, shape, dt))

        res = {
            "iota": t("iota", [P, STRIP]),
            "ident": t("ident", [P, P]),
            "tab": t("tab", [P, sh.NT, 4], I32),
            "bounds": t("bounds", [P, 4, sh.NST + 1], I32),
            "bytile": t("bytile", [1, 5 * sh.NT], I32),
            "colf": t("colf", [P, sh.NT]),
            "coef3": t("coef3", [P, sh.NT, TRI]),
            "gidx": t("gidx", [P, sh.NTG], I32),
            "gcol": t("gcol", [P, sh.NTG]),
            "cself": t("cself", [P, NBLK + 2 * NB]),
            "sdeg_s": t("sdeg_s", [P, NBLK + 2 * NB]),
            "dinv_s": t("dinv_s", [P, NBLK + 2 * NB]),
            "landed": {stage: [ctx.enter_context(nc.semaphore(f"{stage}_landed{k}")) for k in range(n)]
                       for stage, n in (("s", 2), ("a1", RING), ("a2", RING), ("g1", RING), ("g2", RING))},
        }
        build_tables(nc, sh, None, src, dst, edge_type, dram, res)
        build_coefs(nc, sh, dram, res)
        layer(nc, sh, "a1", True, False, x, x, None, dram["h1"], w0[0], b0[0], dram, res)
        layer(nc, sh, "a2", True, True, dram["h1"], dram["h1"], x, dram["x1"], w0[1], b0[1], dram, res)
        layer(nc, sh, "g1", False, False, dram["x1"], dram["x1"], None, dram["hs"], w1, b1, dram, res)
        layer(nc, sh, "g2", False, True, dram["hs"], dram["hs"], dram["x1"], out, w2, b2, dram, res)


_INS = ["x", "src", "dst", "edge_type_9", "L0_gnn_rgcn_weights", "L0_gnn_rgcn_biases",
        "L1_gnn_W1", "L1_gnn_b1", "L1_gnn_W2", "L1_gnn_b2"]


def kernel(**inputs):
    import numpy as np
    import concourse.bacc as bacc
    from concourse.bass_utils import run_bass_kernel_spmd

    nc = bacc.Bacc("TRN2", target_bir_lowering=False, num_devices=1)
    arrays, args = {}, []
    for name in _INS:
        a = np.ascontiguousarray(inputs[name])
        arrays["in_" + name] = a
        args.append(nc.dram_tensor("in_" + name, a.shape, mybir.dt.from_np(a.dtype), kind="ExternalInput").ap())
    n, e = inputs["x"].shape[0], inputs["src"].shape[0]
    sh = Shapes(n, e)
    dram = {
        "table": nc.dram_tensor("dram_table", (P * sh.NT, 4), I32, kind="Internal").ap(),
        "bytile": nc.dram_tensor("dram_bytile", (5, sh.NT), I32, kind="Internal").ap(),
        "cbt": nc.dram_tensor("dram_cbt", (sh.NST, KK + 1, STRIP), FP32, kind="Internal").ap(),
        "h1": nc.dram_tensor("dram_h1", (sh.NST * STRIP, D), FP32, kind="Internal").ap(),
        "x1": nc.dram_tensor("dram_x1", (sh.NST * STRIP, D), FP32, kind="Internal").ap(),
        "hs": nc.dram_tensor("dram_hs", (sh.NST * STRIP, D), FP32, kind="Internal").ap(),
    }
    out = nc.dram_tensor("out", (n, D), FP32, kind="ExternalOutput").ap()
    program(nc, *args, out, dram)
    r = run_bass_kernel_spmd(nc, [arrays], core_ids=[0])
    return r.results[0]["out"]
```

```python
import concourse.bass as bass
from concourse import mybir
from contextlib import ExitStack

FP32 = mybir.dt.float32
BF16 = mybir.dt.bfloat16
FP16 = mybir.dt.float16
I32 = mybir.dt.int32
ALU = mybir.AluOpType
ACT = mybir.ActivationFunctionType
AX = mybir.AxisListType

P = 128
D = 128
STRIP = 512
NB = STRIP // P
R = 9
TRI = 3
NG = R // TRI
KK = 2 * R
SLOTS = 2 * NG
WORDS = 5
FILLS = 8
EPS = 1e-5
FAR = 4096


class Shapes:

    def __init__(self, n, e):
        self.N, self.E = n, e
        self.NST = -(-n // STRIP)
        self.LAST = n - (self.NST - 1) * STRIP
        self.COLS = -(-(-(-e // P)) // 14) * 14
        assert self.COLS * P - e < P and self.COLS <= 256
        self.DBINS = self.NST * NG
        self.NR = -(-(2 * self.NST + 2 * e // P + 4) // FILLS) * FILLS
        assert self.NR < 2048


def col(t, i, n=1):
    return t[:, bass.ds(i, n)]


def within(value, most):
    return value.with_bounds(min_val=1, max_val=most)


def rounds_of(eng, sh, bounds, j):
    v = eng.value_load(bounds[0:1, 0, bass.ds(j, 1)], min_val=1, max_val=sh.NR - 2)
    more = eng.value_load(bounds[0:1, 1, bass.ds(j, 1)], min_val=0, max_val=sh.NR // 2)
    return v, more


def last_round(eng, sh, bounds):
    return eng.value_load(bounds[0:1, 0, sh.NST:sh.NST + 1], min_val=sh.NST + 1, max_val=sh.NR - 2)


def landings(v, slot):
    return v * 8 + 8 if slot == 0 else v * 8


def clear(nc, sems):
    with nc.Block() as block:
        @block.sync
        def _(sp):
            for s in sems:
                sp.sem_clear(s)


def build_tables(nc, sh, src, dst, etype, dram, res):
    NST, COLS, DB, NR = sh.NST, sh.COLS, sh.DBINS, sh.NR
    GRP = 7
    GROUPS = COLS // GRP
    full, rest = sh.E // COLS, sh.E % COLS
    iota, ident, bounds = res["iota"], res["ident"], res["bounds"]
    FROWS = NR // FILLS * SLOTS

    sems = []
    with ExitStack() as ctx:
        def t(name, shape, dt=FP32):
            return ctx.enter_context(nc.sbuf_tensor("s_" + name, shape, dt))

        def sem(name):
            sems.append(ctx.enter_context(nc.semaphore("s_" + name)))
            return sems[-1]

        raw = t("raw", [P, 3, COLS], I32)
        ones = t("ones", [P, P], FP16)
        zero = t("zero", [P, 512], FP16)
        before = t("before", [P, P], FP16)
        row0 = t("row0", [P, P], FP16)
        sums = t("sums", [P, 2, 2, DB + 1], FP16)
        ints = t("ints", [P, 4, COLS], I32)
        flts = t("flts", [P, 7, COLS])
        iota16 = t("iota16", [P, DB + 1], FP16)
        key = t("key", [P, 2, COLS])
        key16 = t("key16", [P, 2, COLS], FP16)
        slot = t("slot", [P, 2, COLS])
        rec = t("rec", [P, 2, COLS, WORDS])
        onehot = t("onehot", [P, 2, 2, GRP, DB + 1], FP16)
        most = t("most", [P, 3, NST])
        mosti = t("mosti", [P, 2, NST], I32)
        rounds = t("rounds", [P, NST])
        incl = t("incl", [P, NST])
        onesrow = t("onesrow", [P, NST])
        start = t("start", [P, DB + 1], FP16)
        junk = t("junk", [P, 2, 2, DB + 1])
        kst = t("kst", [P, 2, 2, GRP])
        posf = t("posf", [P, 2, 2, GRP])
        rows = t("rows", [P, 2, 2, GRP], I32)
        recs = t("recs", [P, 2, 2, GRP, WORDS])
        fill = t("fill", [P, FROWS, WORDS])
        ps_cnt = [ctx.enter_context(nc.psum_tensor(f"s_ps_cnt{d}", [P, 512], FP32)) for d in range(2)]
        ps_pos = [ctx.enter_context(nc.psum_tensor(f"s_ps_pos{d}", [P, 2, 512], FP32)) for d in range(2)]

        raw_cleared, raw_in = sem("raw_cleared"), sem("raw_in")
        consts, fill_ready, filled = sem("consts"), sem("fill_ready"), sem("filled")
        chain, key_ready = sem("chain"), sem("key_ready")
        hot_ready, hist_done = [sem("hot_ready0"), sem("hot_ready1")], [sem("hist_done0"), sem("hist_done1")]
        counted = sem("counted")
        base_ready, hot2_ready = sem("base_ready"), [sem("hot2_ready0"), sem("hot2_ready1")]
        pos_ready, pos_read = [sem("pos_ready0"), sem("pos_ready1")], [sem("pos_read0"), sem("pos_read1")]
        staged, scattered = sem("staged"), res["landed"]["s"]
        sums_ready = [sem("sums_ready0"), sem("sums_ready1")]
        gate, stage_free = sem("gate"), sem("stage_free")
        chain2, staged_parts = sem("chain2"), sem("staged_parts")

        def hot16(d, h):
            out = onehot[:, d, h, :, :]
            return out, iota16[:, :].unsqueeze(1).to_broadcast([P, GRP, DB + 1])

        def keys16(d, g):
            return key16[:, d, bass.ds(g * GRP, GRP)].unsqueeze(2).to_broadcast([P, GRP, DB + 1])

        with nc.Block() as block:
            @block.sync
            def _(sp):
                sp.wait_ge(raw_cleared, 1)
                for i, a in enumerate((src, dst, etype)):
                    sp.dma_start(raw[0:full, i, :], a[0:full * COLS].rearrange("(p c) -> p c", c=COLS)).then_inc(raw_in, 16)
                    if rest:
                        sp.dma_start(raw[full:full + 1, i, 0:rest],
                                     a[full * COLS:sh.E].rearrange("(p c) -> p c", p=1)).then_inc(raw_in, 16)
                sp.wait_ge(fill_ready, 2)
                table = dram["table"].rearrange("(f p t) w -> f p (t w)", f=FILLS, p=P)
                for f in range(FILLS):
                    sp.dma_start(table[f], fill[:, :, :].rearrange("p t w -> p (t w)")).then_inc(filled, 16)
                for h in range(2):
                    sp.wait_ge(scattered[h], 16 * 2 * GRP * (GROUPS // 2))
                sp.wait_ge(filled, 16 * FILLS)

            @block.gpsimd
            def _(pool):
                nc.gpsimd.memset(before[:, :], 1.0).then_inc(consts, 1)
                nc.gpsimd.memset(row0[:, :], float(P)).then_inc(consts, 1)
                nc.gpsimd.memset(ident[:, :], 0.0).then_inc(consts, 1)
                nc.gpsimd.iota(iota[:, :], pattern=[[1, STRIP]], base=0, channel_multiplier=0,
                               allow_small_or_imprecise_dtypes=True).then_inc(consts, 1)
                nc.gpsimd.memset(fill[:, :, :], -1.0).then_inc(consts, 1)
                pool.wait_ge(consts, 5)
                nc.gpsimd.affine_select(out=before[:, :], in_=before[:, :], compare_op=ALU.is_gt, fill=0.0, base=0,
                                        pattern=[[1, P]], channel_multiplier=-1).then_inc(consts, 1)
                nc.gpsimd.affine_select(out=row0[:, :], in_=row0[:, :], compare_op=ALU.is_equal, fill=0.0, base=0,
                                        pattern=[[0, P]], channel_multiplier=1).then_inc(consts, 1)
                nc.gpsimd.affine_select(out=ident[:, :], in_=ident[:, :], compare_op=ALU.not_equal, fill=1.0, base=0,
                                        pattern=[[1, P]], channel_multiplier=-1).then_inc(consts, 1)
                nc.gpsimd.memset(fill[:, :, 0:1], 0.0).then_inc(fill_ready, 2)
                pool.wait_ge(filled, 16 * FILLS)
                with pool.Fori(0, GROUPS // 2) as i:
                    for h in range(2):
                        pool.wait_ge(staged, i * 2 + (h + 1))
                        pool.sem_inc(gate, 1)
                        for d in range(2):
                            for c in range(GRP):
                                nc.gpsimd.indirect_dma_start(
                                    dram["table"], bass.IndirectOffsetOnAxis(ap=rows[:, h, d, c:c + 1], axis=0),
                                    recs[:, h, d, c, :], None).then_inc(scattered[h], 16)
                    for h in range(2):
                        pool.wait_ge(scattered[h], (i + 1) * (16 * 2 * GRP))
                        pool.sem_inc(stage_free, 1)

            @block.vector
            def _(v):
                n = [0]

                def link(ins):
                    n[0] += 1
                    ins.then_inc(chain, 1)
                    v.wait_ge(chain, n[0])

                V = nc.vector
                V.memset(zero[:, :], 0.0)
                V.memset(ones[:, :], 1.0)
                V.memset(sums[:, :, 0, :], 0.0)
                V.memset(onesrow[:, :], 1.0)
                link(V.memset(raw[:, 0:2, :], NST * STRIP))
                V.memset(raw[:, 2, :], 0).then_inc(raw_cleared, 1)
                v.wait_ge(raw_in, 48 * (2 if rest else 1))
                v.wait_ge(consts, 8)
                V.tensor_copy(iota16[:, :], iota[:, 0:DB + 1])
                ty, tg, rel3, a, b, pad, stf = (flts[:, k, :] for k in range(7))
                strip, loc, blk, pp = (ints[:, k, :] for k in range(4))
                link(V.tensor_copy(ty, raw[:, 2, :]))
                link(V.tensor_scalar(a, ty, float(TRI), None, ALU.is_ge))
                link(V.tensor_scalar(b, ty, float(2 * TRI), None, ALU.is_ge))
                link(V.tensor_tensor(tg, a, b, ALU.add))
                link(V.scalar_tensor_tensor(rel3, tg, -float(TRI), ty, ALU.mult, ALU.add))
                for d in range(2):
                    link(V.tensor_scalar(strip, raw[:, d, :], STRIP.bit_length() - 1, None, ALU.logical_shift_right))
                    link(V.tensor_copy(stf, strip))
                    link(V.scalar_tensor_tensor(key[:, d, :], stf, float(NG), tg, ALU.mult, ALU.add))
                    link(V.tensor_copy(key16[:, d, :], key[:, d, :]))
                v.sem_inc(key_ready, 1)

                with v.Fori(0, GROUPS // 2) as i:
                    for h in range(2):
                        for d in range(2):
                            v.wait_ge(hist_done[d], i * 2 + (h + 1))
                            out, i16 = hot16(d, h)
                            V.tensor_tensor(out, i16, keys16(d, i * 2 + h), ALU.is_equal).then_inc(hot_ready[d], 1)
                for d in range(2):
                    node, other = raw[:, d, :], raw[:, 1 - d, :]
                    link(V.tensor_scalar(strip, node, STRIP.bit_length() - 1, None, ALU.logical_shift_right))
                    link(V.tensor_scalar(loc, node, STRIP - 1, None, ALU.bitwise_and))
                    link(V.tensor_scalar(blk, loc, NB - 1, None, ALU.bitwise_and))
                    link(V.tensor_scalar(pp, loc, NB.bit_length() - 1, None, ALU.logical_shift_right))
                    link(V.tensor_copy(stf, strip))
                    link(V.tensor_scalar(slot[:, d, :], tg, float(d * NG), None, ALU.add))
                    link(V.tensor_scalar(pad, stf, float(NST), -float(FAR), ALU.is_ge, ALU.mult))
                    link(V.tensor_scalar(rec[:, d, :, 0].bitcast(I32), other, float(sh.N - 1), None, ALU.min))
                    link(V.scalar_tensor_tensor(a, blk, float(P), pp, ALU.mult, ALU.add))
                    link(V.tensor_tensor(rec[:, d, :, 1], a, pad, ALU.add))
                    link(V.scalar_tensor_tensor(a, blk, float(KK), pad, ALU.mult, ALU.add))
                    link(V.scalar_tensor_tensor(b, ty, 2.0, a, ALU.mult, ALU.add))
                    link(V.tensor_scalar(rec[:, d, :, 2], b, float(d), None, ALU.add))
                    link(V.tensor_copy(rec[:, d, :, 3], rel3))
                    link(V.tensor_tensor(rec[:, d, :, 4], pp, pad, ALU.add))
                v.wait_ge(counted, 1)
                for d in range(2):
                    link(V.tensor_reduce(most[:, d, :], ps_cnt[d][:, 0:DB].rearrange("p (s g) -> p s g", g=NG),
                                         AX.X, ALU.max))
                link(V.tensor_tensor(most[:, 2, :], most[:, 0, :], most[:, 1, :], ALU.max))
                link(V.tensor_scalar(mosti[:, 0, :], most[:, 2, :], float(P - 1), None, ALU.add))
                link(V.tensor_scalar(mosti[:, 1, :], mosti[:, 0, :], 8, None, ALU.logical_shift_right))
                link(V.tensor_copy(bounds[:, 1, 0:NST], mosti[:, 1, :]))
                link(V.tensor_scalar(rounds[:, :], mosti[:, 1, :], 2.0, 1.0, ALU.mult, ALU.add))
                link(V.tensor_tensor_scan(incl[:, :], onesrow[:, :], rounds[:, :], 1.0, ALU.mult, ALU.add))
                link(V.tensor_tensor(most[:, 0, :], incl[:, :], rounds[:, :], ALU.subtract))
                link(V.tensor_copy(bounds[:, 0, 0:NST], most[:, 0, :]))
                link(V.tensor_copy(bounds[:, 0, NST:NST + 1], incl[:, NST - 1:NST]))
                link(V.tensor_copy(start[:, 0:DB].rearrange("p (s g) -> p s g", g=NG),
                                   most[:, 0, :].unsqueeze(2).to_broadcast([P, NST, NG])))
                link(V.tensor_copy(start[:, DB:DB + 1], incl[:, NST - 1:NST]))
                v.sem_inc(base_ready, 1)

                with v.Fori(0, GROUPS // 2) as i:
                    for h in range(2):
                        g = i * 2 + h
                        for d in range(2):
                            v.wait_ge(pos_ready[d], g * GRP + 1)
                            out, i16 = hot16(d, h)
                            V.tensor_tensor(out, i16, keys16(d, g), ALU.is_equal).then_inc(hot2_ready[d], 1)
                        V.tensor_copy(kst[:, h, :, :], key[:, :, bass.ds(g * GRP, GRP)]).then_inc(chain2, 1)
                        v.wait_ge(chain2, g + 1)
                        for c in range(GRP):
                            at = g * GRP + (c + 2)
                            for d in range(2):
                                v.wait_ge(pos_ready[d], at)
                                was, now = (h * GRP + c) % 2, (h * GRP + c + 1) % 2
                                V.tensor_tensor(sums[:, d, now, :], sums[:, d, was, :], onehot[:, d, h, c, :], ALU.add) \
                                    .then_inc(sums_ready[d], 1)
                                V.scalar_tensor_tensor(junk[:, d, was, :], iota[:, 0:DB + 1], kst[:, h, d, c:c + 1],
                                                       ps_pos[d][:, was, 0:DB + 1], ALU.is_equal, ALU.mult,
                                                       accum_out=posf[:, h, d, c:c + 1]).then_inc(pos_read[d], 1)
                        for d in range(2):
                            v.wait_ge(pos_read[d], g * GRP + (GRP + 2))
                        v.wait_ge(stage_free, g + 1)
                        V.scalar_tensor_tensor(rows[:, h, :, :], posf[:, h, :, :], float(SLOTS),
                                               slot[:, :, bass.ds(g * GRP, GRP)], ALU.mult, ALU.add).then_inc(staged_parts, 1)
                        V.tensor_copy(recs[:, h, :, :, :], rec[:, :, bass.ds(g * GRP, GRP), :]).then_inc(staged_parts, 1)
                        v.wait_ge(staged_parts, g * 2 + 2)
                        v.sem_inc(staged, 1)

            @block.scalar
            def _(act):
                for d in range(2):
                    act.sem_inc(hist_done[d], 2)
                    act.sem_inc(pos_ready[d], 1)
                    act.sem_inc(pos_read[d], 2)
                    act.sem_inc(sums_ready[d], 1)
                act.sem_inc(stage_free, 2)

            @block.tensor
            def _(pe):
                pe.wait_ge(consts, 8)
                T = nc.tensor
                pe.wait_ge(key_ready, 1)
                for d in range(2):
                    T.matmul(ps_cnt[d][:, 0:DB + 1], zero[:, 0:P], zero[:, 0:DB + 1], start=True, stop=False)
                with pe.Fori(0, GROUPS // 2) as i:
                    for h in range(2):
                        for d in range(2):
                            pe.wait_ge(hot_ready[d], i * 2 + (h + 1))
                            for c in range(GRP):
                                ins = T.matmul(ps_cnt[d][:, 0:DB + 1], ones[:, :], onehot[:, d, h, c, :],
                                               start=False, stop=False)
                            ins.then_inc(hist_done[d], 1)
                for d in range(2):
                    ins = T.matmul(ps_cnt[d][:, 0:DB + 1], zero[:, 0:P], zero[:, 0:DB + 1], start=False, stop=True)
                ins.then_inc(counted, 1)
                pe.wait_ge(base_ready, 1)
                with pe.Fori(0, GROUPS // 2) as i:
                    for h in range(2):
                        g = i * 2 + h
                        for d in range(2):
                            pe.wait_ge(hot2_ready[d], g + 1)
                        for c in range(GRP):
                            at = g * GRP + (c + 1)
                            for d in range(2):
                                out = ps_pos[d][:, (h * GRP + c) % 2, 0:DB + 1]
                                pe.wait_ge(pos_read[d], at)
                                T.matmul(out, row0[:, :], start[:, :], start=True, stop=False)
                                T.matmul(out, before[:, :], onehot[:, d, h, c, :], start=False, stop=False)
                                pe.wait_ge(sums_ready[d], at)
                                T.matmul(out, ones[:, :], sums[:, d, (h * GRP + c) % 2, :],
                                         start=False, stop=True).then_inc(pos_ready[d], 1)
        clear(nc, sems)


def build_coefs(nc, sh, dram, res):
    NST = sh.NST
    NBLK = NST * NB
    W = NB * KK
    iota, ident, bounds = res["iota"], res["ident"], res["bounds"]
    cself = res["scales"][:, 0:NBLK, 0]
    sdeg, dinv = (res["scales"][:, 2 * NB:2 * NB + NBLK, k] for k in (1, 2))

    sems = []
    with ExitStack() as ctx:
        def t(name, shape, dt=FP32):
            return ctx.enter_context(nc.sbuf_tensor("c_" + name, shape, dt))

        def sem(name):
            sems.append(ctx.enter_context(nc.semaphore("c_" + name)))
            return sems[-1]

        rec = t("rec", [P, 2, SLOTS, WORDS])
        rec2 = t("rec2", [P, 2, SLOTS, WORDS])
        zero = t("zero", [P, P], BF16)
        identb = t("identb", [P, P], BF16)
        hot_p = t("hot_p", [P, 2, SLOTS, P], BF16)
        hot_w = t("hot_w", [P, 2, SLOTS, W], BF16)
        hot_t = t("hot_t", [P, SLOTS, P])
        cnt = t("cnt", [P, NBLK, KK])
        pa = t("pa", [P, NBLK, KK])
        pb = t("pb", [P, NBLK, KK])
        deg = t("deg", [P, NBLK])
        stage = t("stage", [P, 2, NB, KK + 1])
        cbt = t("cbt", [KK + 1, 2, STRIP])
        junk = t("junk", [P, 2, SLOTS, W])
        coef = t("coef", [P, 2, SLOTS])
        wts = t("wts", [P, 2, SLOTS, 1 + TRI])
        ps_cnt = ctx.enter_context(nc.psum_tensor("c_ps_cnt", [P, 2, 512], FP32))
        ps_t = ctx.enter_context(nc.psum_tensor("c_ps_t", [P, 1024], BF16))
        ps_q = ctx.enter_context(nc.psum_tensor("c_ps_q", [P, 2, 512], FP32))

        chain, consts = sem("chain"), sem("consts")
        carried = sem("carried")
        rec_land, rec2_land = [sem("rec_land0"), sem("rec_land1")], [sem("rec2_land0"), sem("rec2_land1")]
        hot_ready, round_mm, closed, cnt_out = sem("hot_ready"), sem("round_mm"), sem("closed"), sem("cnt_out")
        coefs_ready, staged, cb_ps, cb_sb = sem("coefs_ready"), sem("staged"), sem("cb_ps"), sem("cb_sb")
        cb_free, cb_out = sem("cb_free"), [sem("cb_out0"), sem("cb_out1")]
        hp_ready, hp_ps, hp_sb = sem("hp_ready"), sem("hp_ps"), sem("hp_sb")
        q_ps, q_read, wts_ready = sem("q_ps"), sem("q_read"), sem("wts_ready")
        wts_land, wts_free = [sem("wts_land0"), sem("wts_land1")], sem("wts_free")

        table = dram["table"].rearrange("(v p c) w -> v p (c w)", p=P, c=SLOTS)
        weights = dram["weights"].rearrange("(v p c) w -> v p (c w)", p=P, c=SLOTS)

        def one(a, v):
            return a[bass.ds(v, 1), :, :].rearrange("v p n -> (v p) n")

        def one_hot(out, r, s, word, width):
            numbers = iota[:, 0:width].unsqueeze(1).to_broadcast([P, SLOTS, width])
            return nc.vector.tensor_tensor(out, numbers, r[:, s, :, word].unsqueeze(2).to_broadcast([P, SLOTS, width]),
                                           ALU.is_equal)

        def every_round(eng, pair, body):
            for h in range(2):
                v, more = rounds_of(eng, sh, bounds, pair * 2 + h)
                body(v, h, pair * 2 + h, h, True)
                with eng.If(more):
                    with eng.Fori(0, more) as i:
                        body(within(v + i * 2 + 1, sh.NR - 3), 1 - h, pair * 2 + h, h, False)
                        body(within(v + i * 2 + 2, sh.NR - 3), h, pair * 2 + h, h, False)

        with nc.Block() as block:
            @block.sync
            def _(sp):
                def row(r, land, v, s):
                    sp.dma_start(r[:, s, :, :].rearrange("p c w -> p (c w)"), one(table, v)).then_inc(land[s], 16)

                for v in (1, 2):
                    row(rec, rec_land, v, v - 1)
                    row(rec2, rec2_land, v, v - 1)

                def counting(v, s, j, h, main):
                    sp.wait_ge(hot_ready, v)
                    sp.sem_inc(carried, 1)
                    row(rec, rec_land, within(v + 2, sh.NR - 1), s)

                with sp.Fori(0, NST // 2) as pair:
                    every_round(sp, pair, counting)
                with sp.Fori(0, NST // 2) as pair:
                    j = pair * 2
                    for h in range(2):
                        sp.wait_ge(cb_sb, j + (h + 1))
                        sp.dma_start(dram["cbt"][bass.ds(j + h, 1), :, :].rearrange("s k n -> (s k) n"),
                                     cbt[:, h, :]).then_inc(cb_out[h], 16)
                        sp.wait_ge(cb_out[h], j * 8 + 16)
                        sp.sem_inc(cb_free, 1)

                def weighing(v, s, j, h, main):
                    sp.wait_ge(wts_ready, v)
                    sp.sem_inc(carried, 1)
                    sp.dma_start(one(weights, v), wts[:, s, :, :].rearrange("p c w -> p (c w)")).then_inc(wts_land[s], 16)
                    row(rec2, rec2_land, within(v + 2, sh.NR - 1), s)
                    sp.wait_ge(wts_land[s], landings(v, s))
                    sp.sem_inc(wts_free, 1)

                with sp.Fori(0, NST // 2) as pair:
                    every_round(sp, pair, weighing)
                end = last_round(sp, sh, bounds)
                for k in range(2):
                    sp.dma_start(one(weights, within(end + k, sh.NR - 1)),
                                 wts[:, k, :, :].rearrange("p c w -> p (c w)")).then_inc(wts_land[k], 16)
                for k in range(2):
                    sp.wait_ge(wts_land[k], landings(end + k, k))
                    sp.wait_ge(rec_land[k], landings(end + k, k))
                    sp.wait_ge(rec2_land[k], landings(end + k, k))
                    sp.sem_inc(carried, 1)

            @block.vector
            def _(v_):
                n = [0]
                V = nc.vector

                def link(ins):
                    n[0] += 1
                    ins.then_inc(chain, 1)
                    v_.wait_ge(chain, n[0])

                V.memset(res["scales"][:, :, 0:1], 0.0)
                V.memset(res["scales"][:, :, 1:3], 1.0)
                V.memset(zero[:, :], 0.0)
                link(V.tensor_copy(identb[:, :], ident[:, :]))
                v_.sem_inc(consts, 1)

                def counting(v, s, j, h, main):
                    v_.wait_ge(rec_land[s], landings(v, s))
                    v_.wait_ge(round_mm, v)
                    one_hot(hot_p[:, s, :, :], rec, s, 4, P)
                    one_hot(hot_w[:, s, :, :], rec, s, 2, W).then_inc(hot_ready, 1)

                with v_.Fori(0, NST // 2) as pair:
                    every_round(v_, pair, counting)
                v_.wait_ge(cnt_out, NST + 2)
                link(V.tensor_scalar(pa[:, :, :], cnt[:, :, :], 1.0, None, ALU.max))
                link(V.reciprocal(pb[:, :, :], pa[:, :, :]))
                link(V.tensor_scalar(pa[:, :, :], pb[:, :, :], 2.0, None, ALU.mult))
                a, b = pa, pb
                s = 1
                while s < KK:
                    V.tensor_tensor(b[:, :, 0:KK - s], a[:, :, 0:KK - s], a[:, :, s:KK], ALU.mult)
                    link(V.tensor_copy(b[:, :, KK - s:KK], a[:, :, KK - s:KK]))
                    a, b = b, a
                    s *= 2
                assert a is pb
                link(V.tensor_copy(cself, pb[:, :, 0]))
                link(V.tensor_reduce(deg[:, :], cnt[:, :, :].rearrange("p b (r d) -> p b d r", d=2)[:, :, 1, :],
                                     AX.X, ALU.add))
                link(V.tensor_scalar(deg[:, :], deg[:, :], 1.0, None, ALU.add))
                v_.sem_inc(coefs_ready, 1)
                v_.wait_ge(coefs_ready, 2)
                link(V.reciprocal(dinv, sdeg))
                link(V.tensor_tensor(pa[:, :, :], cnt[:, :, :], pb[:, :, :], ALU.mult))
                with v_.Fori(0, NST // 2) as pair:
                    j = pair * 2
                    for h in range(2):
                        v_.wait_ge(cb_ps, j + (h + 1))
                        b0 = (j + h) * NB
                        V.tensor_copy(stage[:, h, :, 0:KK], pa[:, bass.ds(b0, NB), :])
                        V.tensor_copy(stage[:, h, :, KK:KK + 1], pb[:, bass.ds(b0, NB), 0:1]).then_inc(staged, 1)

                def turned(v, s):
                    v_.wait_ge(rec2_land[s], landings(v, s))
                    one_hot(hot_p[:, s, :, :], rec2, s, 4, P).then_inc(hp_ready, 1)

                def weighing(v, s, j, h, main):
                    turned(within(v + 1, sh.NR - 2), 1 - s)
                    v_.wait_ge(q_ps, v)
                    for c in range(SLOTS):
                        V.scalar_tensor_tensor(junk[:, s, c, :], iota[:, 0:W], rec2[:, s, c, 2:3],
                                               ps_q[:, s, c * W:c * W + W], ALU.is_equal, ALU.mult,
                                               accum_out=coef[:, s, c:c + 1]).then_inc(q_read, 1)
                    v_.wait_ge(wts_free, v)
                    V.tensor_copy(wts[:, s, :, 0], rec2[:, s, :, 1])
                    v_.wait_ge(q_read, v * SLOTS)
                    for i in range(TRI):
                        ins = V.scalar_tensor_tensor(wts[:, s, :, 1 + i], rec2[:, s, :, 3], float(i), coef[:, s, :],
                                                     ALU.is_equal, ALU.mult)
                    ins.then_inc(wts_ready, 1)

                turned(1, 0)
                with v_.Fori(0, NST // 2) as pair:
                    every_round(v_, pair, weighing)

            @block.scalar
            def _(act):
                act.sem_inc(round_mm, 2)
                act.sem_inc(cnt_out, 2)
                act.sem_inc(cb_ps, 1)
                act.sem_inc(cb_free, 2)
                act.sem_inc(wts_free, 2)
                C = nc.scalar
                with act.Fori(0, NST // 2) as pair:
                    for h in range(2):
                        j = pair * 2 + h
                        act.wait_ge(closed, j + 1)
                        C.activation(cnt[:, bass.ds(j * NB, NB), :].rearrange("p b k -> p (b k)"),
                                     ps_cnt[:, h, 0:W], ACT.Copy).then_inc(cnt_out, 1)
                act.wait_ge(coefs_ready, 1)
                C.activation(sdeg, deg[:, :], ACT.Sqrt).then_inc(coefs_ready, 1)
                with act.Fori(0, NST // 2) as pair:
                    j = pair * 2
                    for h in range(2):
                        act.wait_ge(cb_ps, j + (h + 2))
                        act.wait_ge(cb_free, j + (h + 1))
                        C.activation(cbt[:, h, :], ps_cnt[0:KK + 1, h, :], ACT.Copy).then_inc(cb_sb, 1)

                def weighing(v, s, j, h, main):
                    act.wait_ge(hp_ps, v)
                    C.activation(hot_t[:, :, :].rearrange("p k m -> p (k m)"), ps_t[:, 0:SLOTS * P], ACT.Copy) \
                        .then_inc(hp_sb, 1)

                with act.Fori(0, NST // 2) as pair:
                    every_round(act, pair, weighing)

            @block.tensor
            def _(pe):
                M = nc.tensor
                pe.wait_ge(consts, 1)

                def counting(v, s, j, h, main):
                    if main:
                        pe.wait_ge(cnt_out, j + 1)
                    pe.wait_ge(hot_ready, v)
                    for c in range(SLOTS):
                        ins = M.matmul(ps_cnt[:, h, 0:W], hot_p[:, s, c, :], hot_w[:, s, c, :],
                                       start=main and c == 0, stop=False)
                    ins.then_inc(round_mm, 1)

                with pe.Fori(0, NST // 2) as pair:
                    for h in range(2):
                        j = pair * 2 + h
                        v, more = rounds_of(pe, sh, bounds, j)
                        counting(v, h, j, h, True)
                        with pe.If(more):
                            with pe.Fori(0, more) as i:
                                counting(within(v + i * 2 + 1, sh.NR - 3), 1 - h, j, h, False)
                                counting(within(v + i * 2 + 2, sh.NR - 3), h, j, h, False)
                        M.matmul(ps_cnt[:, h, 0:W], zero[:, :], zero[:, 0:W], start=False, stop=True).then_inc(closed, 1)
                with pe.Fori(0, NST // 2) as pair:
                    j = pair * 2
                    for h in range(2):
                        pe.wait_ge(staged, j + (h + 1))
                        pe.wait_ge(cb_free, j + (h + 1))
                        for b in range(NB):
                            ins = M.transpose(ps_cnt[0:KK + 1, h, b * P:b * P + P], stage[:, h, b, :], ident[:, :])
                        ins.then_inc(cb_ps, 1)

                def weighing(v, s, j, h, main):
                    pe.wait_ge(hp_ready, v)
                    for c in range(SLOTS):
                        ins = M.transpose(ps_t[:, c * P:c * P + P], hot_p[:, s, c, :], identb[:, :])
                    ins.then_inc(hp_ps, 1)
                    pe.wait_ge(hp_sb, v)
                    for c in range(SLOTS):
                        ins = M.matmul(ps_q[:, s, c * W:c * W + W], hot_t[:, c, :],
                                       pb[:, bass.ds(j * NB, NB), :].rearrange("p b k -> p (b k)"),
                                       start=True, stop=True)
                    ins.then_inc(q_ps, 1)

                with pe.Fori(0, NST // 2) as pair:
                    every_round(pe, pair, weighing)
        clear(nc, sems)


def layer(nc, sh, name, rgcn, last, gathered, own, residual, to, weights, bias, dram, res):
    NST = sh.NST
    iota, ident, bounds, scales = res["iota"], res["ident"], res["bounds"], res["scales"]
    S = SLOTS if rgcn else NG
    C0 = SLOTS - S
    SB = 1 if rgcn else 2
    CONSTS = 9

    sems = []
    with ExitStack() as ctx:
        def t(n_, shape, dt=FP32):
            return ctx.enter_context(nc.sbuf_tensor(f"{name}_{n_}", shape, dt))

        def ps(n_, shape):
            return ctx.enter_context(nc.psum_tensor(f"{name}_{n_}", shape, FP32))

        def sem(n_):
            sems.append(ctx.enter_context(nc.semaphore(f"{name}_{n_}")))
            return sems[-1]

        def sems_of(n_, count):
            return [sem(f"{n_}{k}") for k in range(count)]

        rec = t("rec", [P, 2, SLOTS, WORDS])
        wts = t("wts", [P, 2, SLOTS, 1 + TRI])
        xg = t("xg", [P, 2, S, D])
        xin = t("xin", [P, 2, STRIP])
        xres = t("xres", [P, 2, STRIP])
        sc = t("sc", [P, 2, NB, 3])
        xc = t("xc", [P, STRIP])
        xt = t("xt", [D, STRIP])
        ht = t("ht", [D, STRIP])
        sel = t("sel", [P, SB, S, STRIP])
        outb = t("outb", [P, 2, STRIP])
        eps = t("eps", [P, 1])
        if rgcn:
            wall = t("wall", [D, KK * D])
            wself = t("wself", [D, D])
            ball = t("ball", [KK + 1, D])
            cb = t("cb", [KK + 1, 2, STRIP])
            turned = t("turned", [P, S, P])
            part = t("part", [P, S, D])
            mid = t("mid", [P, S, D])
            y = t("y", [P, S, D])
            ps_xt = ps("ps_xt", [P, 2, 512])
            ps_y = ps("ps_y", [P, 2, 512])
        else:
            wgcn = t("wgcn", [D, D])
            brow = t("brow", [P, D])
        z = t("z", [P, STRIP])
        if last:
            stats = t("stats", [P, NB, 6])
            mv = t("mv", [P, NB, 2])
            sd = t("sd", [P, NB])
            rs = t("rs", [P, NB])
            rs2 = t("rs2", [P, NB])
        if not rgcn:
            za = t("za", [P, STRIP])
            zb = t("zb", [P, STRIP])
        ps_h = ps("ps_h", [P, 2, STRIP])
        ps_x = ps("ps_x", [P, STRIP])
        ps_o = ps("ps_o", [P, STRIP])

        landed = res["landed"][name]
        w_in, consts, gate = sem("w_in"), sem("consts"), sem("gate")
        carried = sem("carried")
        rec_land, wts_land = sems_of("rec_land", 2), sems_of("wts_land", 2)
        sel_sb, used = sems_of("sel_sb", S), sems_of("used", S)
        if rgcn:
            xt_ps, xt_sb = sems_of("xt_ps", S), sems_of("xt_sb", S)
            y_ps, part_sb, mid_sb, y_sb = (sems_of(n_, S) for n_ in ("y_ps", "part_sb", "mid_sb", "y_sb"))
            cb_land, xc_sb = sems_of("cb_land", 2), sem("xc_sb")
        in_land, res_land, st_land = sems_of("in_land", 2), sems_of("res_land", 2), sems_of("st_land", 2)
        closed = sem("closed")
        sc_sb, own_ps, own_sb = sem("sc_sb"), sem("own_ps"), sem("own_sb")
        ht_sb, out_ps, out_read = sem("ht_sb"), sem("out_ps"), sem("out_read")
        res_ready, res_read, out_free = sem("res_ready"), sem("res_read"), sem("out_free")
        fin = sem("fin")
        passed, var_ready, sd_ready = sem("passed"), sem("var_ready"), sem("sd_ready")
        fin_links = sems_of("fin_link", 6)

        def strip_rows(a, j, n_rows=STRIP):
            start = j * STRIP
            rows = a[start:start + n_rows, :] if isinstance(j, int) else a[bass.ds(start, n_rows), :]
            return rows.rearrange("(p b) d -> p (b d)", b=NB)

        def strip_parts(j):
            return sh.LAST // NB if isinstance(j, int) and j == NST - 1 else P

        with nc.Block() as block:
            @block.gpsimd
            def _(pool):
                def gather(v, s, c):
                    pool.wait_ge(used[c], v)
                    pool.sem_inc(gate, 1)
                    nc.gpsimd.indirect_dma_start(
                        xg[:, s, c, :], None, gathered[0:sh.N, :],
                        bass.IndirectOffsetOnAxis(ap=rec[:, s, C0 + c, 0:1].bitcast(I32), axis=0)) \
                        .then_inc(landed[s][c], 16)

                def round_(v, s):
                    pool.wait_ge(rec_land[s], landings(v, s))
                    for c in range(S):
                        gather(v, s, c)

                with pool.Fori(0, NST // 2) as pair:
                    for h in range(2):
                        v, more = rounds_of(pool, sh, bounds, pair * 2 + h)
                        round_(v, h)
                        with pool.If(more):
                            with pool.Fori(0, more) as i:
                                round_(within(v + i * 2 + 1, sh.NR - 3), 1 - h)
                                round_(within(v + i * 2 + 2, sh.NR - 3), h)
                if rgcn:
                    end = last_round(pool, sh, bounds)
                    pool.wait_ge(rec_land[0], landings(end, 0))
                    for c in range(2):
                        gather(end, 0, c)

            @block.sync
            def _(sp):
                if rgcn:
                    for d in range(2):
                        sp.dma_start(wall[:, d * R * D:(d + 1) * R * D].rearrange("k (r m) -> k r m", m=D),
                                     weights[d * R:(d + 1) * R, :, :].rearrange("r k m -> k r m")).then_inc(w_in, 16)
                        sp.dma_start(ball[d:KK:2, :], bias[d * R:(d + 1) * R, :]).then_inc(w_in, 16)
                    sp.dma_start(wself[:, :], weights[KK, :, :]).then_inc(w_in, 16)
                    sp.dma_start(ball[KK:KK + 1, :], bias[KK:KK + 1, :]).then_inc(w_in, 16)
                else:
                    sp.dma_start(wgcn[:, :], weights).then_inc(w_in, 16)
                    sp.dma_start(brow[:, :], bias.rearrange("(o d) -> o d", o=1).to_broadcast([P, D])).then_inc(w_in, 16)

                def table_row(a, tile, v):
                    rows = dram[a].rearrange("(v p c) w -> v p (c w)", p=P, c=SLOTS)
                    return rows[bass.ds(v, 1), :, :].rearrange("v p n -> (v p) n")

                def load_rec(v, s):
                    sp.dma_start(rec[:, s, :, :].rearrange("p c w -> p (c w)"), table_row("table", rec, v)) \
                        .then_inc(rec_land[s], 16)

                def load_wts(v, s):
                    sp.dma_start(wts[:, s, :, :].rearrange("p c w -> p (c w)"), table_row("weights", wts, v)) \
                        .then_inc(wts_land[s], 16)

                def load_own(j, h):
                    sp.dma_start(xin[0:strip_parts(j), h, :], strip_rows(own, j, strip_parts(j) * NB)).then_inc(in_land[h], 16)

                def load_cb(j, h):
                    sp.dma_start(cb[:, h, :], dram["cbt"][bass.ds(j, 1), :, :].rearrange("s k n -> (s k) n")) \
                        .then_inc(cb_land[h], 16)

                def load_res(j, h):
                    sp.dma_start(xres[0:strip_parts(j), h, :], strip_rows(residual, j, strip_parts(j) * NB)) \
                        .then_inc(res_land[h], 16)

                def rec_ahead(v, s):
                    for c in range(S):
                        sp.wait_ge(landed[s][c], landings(v, s))
                    sp.sem_inc(carried, 1)
                    load_rec(within(v + 2, sh.NR - 1), s)

                def wts_ahead(v, s):
                    sp.wait_ge(used[S - 1], v + 2)
                    sp.sem_inc(carried, 1)
                    load_wts(within(v + 2, sh.NR - 1), s)

                def strip_dmas(j, h):
                    if not isinstance(j, int) or j + 2 < NST:
                        sp.wait_ge(xc_sb if rgcn else own_ps, j + (1 if rgcn else 2))
                        sp.sem_inc(carried, 1)
                        load_own(j + 2, h)
                    if rgcn and (not isinstance(j, int) or 1 <= j < NST - 1):
                        sp.wait_ge(closed, j + 1)
                        sp.sem_inc(carried, 1)
                        load_cb(j + 1, 1 - h)
                    if last and (not isinstance(j, int) or 1 <= j <= NST):
                        sp.wait_ge(res_read, j)
                        sp.sem_inc(carried, 1)
                        load_res(j - 1, 1 - h)
                    if not isinstance(j, int) or 3 <= j:
                        k = j - 3
                        sp.wait_ge(fin, k + 5)
                        sp.sem_inc(carried, 1)
                        sp.dma_start(strip_rows(to, k, strip_parts(k) * NB), outb[0:strip_parts(k), 1 - h, :]) \
                            .then_inc(st_land[1 - h], 16)

                def relay(j, h):
                    if last and (not isinstance(j, int) or 1 <= j <= NST):
                        sp.wait_ge(res_land[1 - h], (j - 1 - (1 - h)) * 8 + 16)
                        sp.sem_inc(res_ready, 1)
                    if not isinstance(j, int) or j >= 3:
                        sp.wait_ge(st_land[1 - h], (j - 3 - (1 - h)) * 8 + 16)
                        sp.sem_inc(out_free, 1)

                def step(j, h):
                    v, more = rounds_of(sp, sh, bounds, j)
                    rec_ahead(v, h)
                    strip_dmas(j, h)
                    relay(j, h)
                    wts_ahead(v, h)
                    with sp.If(more):
                        with sp.Fori(0, more) as i:
                            for k, s in ((1, 1 - h), (2, h)):
                                u = within(v + i * 2 + k, sh.NR - 3)
                                rec_ahead(u, s)
                                wts_ahead(u, s)

                sp.wait_ge(consts, CONSTS)
                for k in range(2):
                    load_rec(k + 1, k)
                    load_wts(k + 1, k)
                    load_own(k, k)
                    if rgcn:
                        load_cb(k, k)
                for j in range(4):
                    step(j, j % 2)
                with sp.Fori(2, (NST - 4) // 2) as pair:
                    for h in range(2):
                        step(pair * 2 + h, h)
                for j in range(NST - 4, NST):
                    step(j, j % 2)
                for j in range(NST, NST + 3):
                    strip_dmas(j, j % 2)
                    relay(j, j % 2)
                end = last_round(sp, sh, bounds)
                for k in range(2):
                    sp.wait_ge(st_land[k], (NST // 2) * 16)
                    sp.wait_ge(rec_land[k], landings(end + k, k))
                    sp.wait_ge(wts_land[k], landings(end + k, k))
                    sp.sem_inc(carried, 1)

            @block.vector
            def _(v_):
                V = nc.vector
                V.memset(ps_h[:, 1, :], 0.0).then_inc(consts, 1)
                V.memset(ps_o[:, :], 0.0).then_inc(consts, 1)
                V.memset(ht[:, :], 0.0).then_inc(consts, 1)
                V.memset(outb[:, :, :], 0.0).then_inc(consts, 1)
                V.memset(xin[:, :, :], 0.0).then_inc(consts, 1)
                V.memset(eps[:, :], EPS).then_inc(consts, 1)
                V.memset(xres[:, :, :], 0.0).then_inc(consts, 1)
                V.memset(z[:, :], 0.0).then_inc(consts, 1)
                V.memset(xt[:, :], 0.0).then_inc(consts, 1)
                v_.wait_ge(consts, CONSTS)
                v_.sem_inc(res_ready, 2)
                v_.sem_inc(out_free, 4)
                for c in range(S):
                    v_.sem_inc(used[c], 2)
                v_.sem_inc(closed, 1)
                v_.sem_inc(out_ps, 1)
                v_.sem_inc(own_ps, 1)
                v_.sem_inc(fin, 2)
                v_.wait_ge(w_in, 96 if rgcn else 32)

                def selection(v, s, c):
                    w = wts[:, s, C0 + c, 0:1]
                    if rgcn:
                        v_.wait_ge(used[c], v + 1)
                        V.tensor_scalar(sel[:, 0, c, :], iota[:, :], w, None, ALU.is_equal).then_inc(sel_sb[c], 1)
                    else:
                        v_.wait_ge(used[c], v)
                        V.tensor_scalar(sel[:, s, c, :], iota[:, :], w, None, ALU.is_equal).then_inc(sel_sb[c], 1)

                def weighted(v, s, c):
                    prods, w = ps_y[:, c % 2, :], wts[:, s, c, :]
                    v_.wait_ge(part_sb[c], v)
                    V.scalar_tensor_tensor(mid[:, c, :], prods[:, D:2 * D], w[:, 2:3], part[:, c, :],
                                           ALU.mult, ALU.add).then_inc(mid_sb[c], 1)
                    v_.wait_ge(mid_sb[c], v)
                    V.scalar_tensor_tensor(y[:, c, :], prods[:, 2 * D:3 * D], w[:, 3:4], mid[:, c, :],
                                           ALU.mult, ALU.add).then_inc(y_sb[c], 1)

                def round_(v, s, steps):
                    for c in range(S):
                        if rgcn:
                            weighted(v, s, c)
                        if c < S - 1:
                            selection(v, s, c + 1)
                        else:
                            v_.wait_ge(wts_land[1 - s], landings(v + 1, 1 - s))
                            selection(v + 1, 1 - s, 0)
                        for f in steps[c] if c < len(steps) else []:
                            f()

                def blocks(a):
                    return [a[:, b * D:b * D + D] for b in range(NB)]

                def finish(h, one):
                    dst, xr = outb[:, h, :], xres[:, h, :]
                    sq, di = ([sc[:, h, b, i:i + 1] for b in range(NB)] for i in (1, 2))

                    def after(i):
                        v_.wait_ge(fin_links[i], one)

                    def take():
                        v_.wait_ge(out_ps, one)
                        v_.wait_ge(sc_sb, one)
                        if rgcn and not last:
                            v_.wait_ge(out_free, one)
                            V.tensor_scalar(dst, ps_o[:, :], 0.0, None, ALU.max).then_inc(out_read, 1)
                            v_.wait_ge(out_read, one)
                            v_.sem_inc(fin, 1)
                        elif rgcn:
                            v_.wait_ge(res_ready, one)
                            V.tensor_tensor(z[:, :], ps_o[:, :], xr, ALU.add).then_inc(out_read, 1)
                        else:
                            v_.wait_ge(fin, one + 1)
                            for b in range(NB):
                                ins = V.scalar_tensor_tensor(blocks(za)[b], blocks(ps_o)[b], di[b], brow[:, :], ALU.mult, ALU.add)
                            ins.then_inc(out_read, 1)

                    def rows_out():
                        v_.wait_ge(out_read, one)
                        v_.wait_ge(out_free, one)
                        for b in range(NB):
                            ins = V.tensor_scalar(blocks(dst)[b], blocks(za)[b], 0.0, di[b], ALU.max, ALU.mult)
                        ins.then_inc(fin, 1)

                    def add_residual():
                        v_.wait_ge(out_read, one)
                        V.tensor_scalar(zb[:, :], za[:, :], 0.0, None, ALU.max).then_inc(fin_links[0], 1)
                        v_.wait_ge(res_ready, one)
                        after(0)
                        for b in range(NB):
                            ins = V.scalar_tensor_tensor(blocks(z)[b], blocks(xr)[b], sq[b], blocks(zb)[b], ALU.mult, ALU.add)
                        ins.then_inc(fin_links[1], 1)

                    def statistics():
                        if rgcn:
                            v_.wait_ge(out_read, one)
                        else:
                            after(1)
                        v_.sem_inc(res_read, 1)
                        for b in range(NB):
                            ins = V.bn_stats(stats[:, b, :], blocks(z)[b])
                        ins.then_inc(fin_links[2], 1)

                    def variance():
                        after(2)
                        v_.sem_inc(passed, 1)
                        for b in range(NB):
                            ins = V.bn_aggr(mv[:, b, :], stats[:, b, :])
                        ins.then_inc(var_ready, 1)

                    def inverse():
                        v_.wait_ge(sd_ready, one)
                        V.reciprocal(rs[:, :], sd[:, :]).then_inc(fin_links[3], 1)
                        after(3)
                        if rgcn:
                            V.tensor_tensor(rs2[:, :], rs[:, :], sc[:, h, :, 2], ALU.mult).then_inc(fin_links[4], 1)
                        else:
                            V.tensor_copy(rs2[:, :], rs[:, :]).then_inc(fin_links[4], 1)

                    def normalize():
                        after(4)
                        v_.wait_ge(out_free, one)
                        for b in range(NB):
                            ins = V.tensor_scalar(blocks(dst)[b], blocks(z)[b], mv[:, b, 0:1], rs2[:, b:b + 1],
                                                  ALU.subtract, ALU.mult)
                        ins.then_inc(fin, 1)

                    if rgcn:
                        return [[], [take], [statistics], [variance], [], [inverse, normalize]] if last else [[], [], [take]]
                    return [[take, add_residual], [statistics, variance], [inverse, normalize]] if last else [[take], [rows_out]]

                v_.wait_ge(wts_land[0], 16)
                selection(1, 0, 0)
                with v_.Fori(0, NST // 2) as pair:
                    for h in range(2):
                        v, more = rounds_of(v_, sh, bounds, pair * 2 + h)
                        steps = finish(h, pair * 2 + (h + 1))
                        round_(v, h, steps)
                        with v_.If(more):
                            with v_.Fori(0, more) as i:
                                for k, s in ((1, 1 - h), (2, h)):
                                    u = within(v + i * 2 + k, sh.NR - 3)
                                    round_(u, s, [])
                for j in (NST, NST + 1):
                    v_.wait_ge(fin, j + 2)
                    for step in finish(j % 2, j + 1):
                        for f in step:
                            f()

            @block.scalar
            def _(act):
                C = nc.scalar
                act.wait_ge(consts, CONSTS)

                def turned_copy(v, c):
                    act.wait_ge(xt_ps[c], v)
                    C.activation(turned[:, c, :], ps_xt[:, c % 2, 0:P], ACT.Copy).then_inc(xt_sb[c], 1)

                def first_part(v, s, c):
                    act.wait_ge(y_ps[c], v)
                    C.activation(part[:, c, :], ps_y[:, c % 2, 0:D], ACT.Copy, scale=wts[:, s, c, 1:2]).then_inc(part_sb[c], 1)

                def node_scales(j, h):
                    act.wait_ge(fin, j + 1)
                    C.activation(sc[:, h, :, :], scales[:, bass.ds(j * NB, NB), :], ACT.Copy).then_inc(sc_sb, 1)

                def own_rows(j, h, x16, part_):
                    if part_ == 0:
                        act.wait_ge(sc_sb, j + 1)
                        act.wait_ge(in_land[h], x16)
                        act.wait_ge(own_ps, j + 1)
                    for b in range(part_ * NB // 2, (part_ + 1) * NB // 2):
                        ins = C.activation(xc[:, b * D:b * D + D], xin[:, h, b * D:b * D + D], ACT.Copy, scale=sc[:, h, b, 0:1])
                    if part_ == 1:
                        ins.then_inc(xc_sb, 1)

                def own_turned(j):
                    act.wait_ge(own_ps, j + 2)
                    C.activation(xt[:, :], ps_x[:, :], ACT.Copy).then_inc(own_sb, 1)

                def hidden(j, h):
                    act.wait_ge(out_ps, j + 1)
                    act.wait_ge(closed, j + 1)
                    C.activation(ht[:, :], ps_h[:, 1 - h, :], ACT.Copy).then_inc(ht_sb, 1)

                def deviation(j):
                    act.wait_ge(var_ready, j + 1)
                    C.activation(sd[:, :], mv[:, :, 1], ACT.Sqrt, bias=eps[:, 0:1]).then_inc(sd_ready, 1)

                def round_(v, s, nxt, j=None, x16=None):
                    for c in range(S):
                        if rgcn:
                            u, cc = (v, c + 2) if c + 2 < S else (nxt, c + 2 - S)
                            turned_copy(u, cc)
                            if c == S - 1:
                                act.wait_ge(wts_land[1 - s], landings(nxt, 1 - s))
                                first_part(nxt, 1 - s, 0)
                            else:
                                first_part(v, s, c + 1)
                        if j is None:
                            continue
                        if rgcn and c == 0:
                            node_scales(j, s)
                            hidden(j, s)
                        if rgcn and c in (1, 2):
                            own_rows(j, s, x16, c - 1)
                        if not rgcn and c == 0:
                            node_scales(j, s)
                            hidden(j, s)
                            own_turned(j)
                        if rgcn and c == 4:
                            own_turned(j)
                        if last and c == (4 if rgcn else 1):
                            deviation(j)

                if rgcn:
                    turned_copy(1, 0)
                    turned_copy(1, 1)
                    act.wait_ge(wts_land[0], 16)
                    first_part(1, 0, 0)
                with act.Fori(0, NST // 2) as pair:
                    for h in range(2):
                        if rgcn:
                            v, more = rounds_of(act, sh, bounds, pair * 2 + h)
                            round_(v, h, v + 1, pair * 2 + h, pair * 16 + 16)
                            with act.If(more):
                                with act.Fori(0, more) as i:
                                    for k, s in ((1, 1 - h), (2, h)):
                                        u = within(v + i * 2 + k, sh.NR - 3)
                                        round_(u, s, u + 1)
                        else:
                            round_(None, h, None, pair * 2 + h, None)
                hidden(NST, 0)
                node_scales(NST, 0)
                if last:
                    deviation(NST)
                node_scales(NST + 1, 1)
                if last:
                    deviation(NST + 1)

            @block.tensor
            def _(pe):
                M = nc.tensor
                pe.wait_ge(w_in, 96 if rgcn else 32)
                pe.wait_ge(consts, CONSTS)

                def turn_tile(v, s, c):
                    pe.wait_ge(landed[s][c], landings(v, s))
                    M.transpose(ps_xt[:, c % 2, 0:P], xg[:, s, c, :], ident[:, :]).then_inc(xt_ps[c], 1)

                def product(v, c):
                    pe.wait_ge(xt_sb[c], v)
                    M.matmul(ps_y[:, c % 2, 0:TRI * D], turned[:, c, :], wall_of(c), start=True, stop=True).then_inc(y_ps[c], 1)

                def wall_of(c):
                    off = (c // NG * R + c % NG * TRI) * D
                    return wall[:, off:off + TRI * D]

                def own_turn(j, h, x16):
                    if rgcn:
                        pe.wait_ge(xc_sb, j + 1)
                    else:
                        pe.wait_ge(in_land[h], x16)
                    src = xc[:, :] if rgcn else xin[:, h, :]
                    for b in range(NB):
                        ins = M.transpose(ps_x[:, b * P:b * P + P], src[:, b * D:b * D + D], ident[:, :])
                    ins.then_inc(own_ps, 1)

                def out(j):
                    pe.wait_ge(ht_sb, j + 1)
                    pe.wait_ge(out_read, j + 1)
                    for b in range(NB):
                        dst, hb = ps_o[:, b * D:b * D + D], ht[:, b * P:b * P + P]
                        ins = M.transpose(dst, hb, ident[:, :]) if rgcn else M.matmul(dst, hb, wgcn[:, :], start=True, stop=True)
                    ins.then_inc(out_ps, 1)

                def close(j, h, x16):
                    pe.wait_ge(own_sb, j + 1)
                    acc = ps_h[:, h, :]
                    if rgcn:
                        pe.wait_ge(cb_land[h], x16)
                        M.matmul(acc, ball[:, :], cb[:, h, :], start=False, stop=False)
                        M.matmul(acc, wself[:, :], xt[:, :], start=False, stop=True).then_inc(closed, 1)
                    else:
                        M.matmul(acc, ident[:, :], xt[:, :], start=False, stop=True).then_inc(closed, 1)

                def round_(v, s, nxt, h, j=None, x16=None):
                    for c in range(S):
                        if rgcn:
                            u, us, cc = (v, s, c + 2) if c + 2 < S else (nxt, 1 - s, c + 2 - S)
                            turn_tile(u, us, cc)
                            u, cc = (v, c + 1) if c + 1 < S else (nxt, 0)
                            product(u, cc)
                            pe.wait_ge(y_sb[c], v)
                            lhs, selected = y[:, c, :], sel[:, 0, c, :]
                        else:
                            pe.wait_ge(landed[s][c], landings(v, s))
                            pe.wait_ge(sel_sb[c], v)
                            lhs, selected = xg[:, s, c, :], sel[:, s, c, :]
                        M.matmul(ps_h[:, h, :], lhs, selected, start=j is not None and c == 0, stop=False).then_inc(used[c], 1)
                        if j is None:
                            continue
                        if c == (4 if rgcn else 0):
                            own_turn(j, h, x16)
                        if c == (5 if rgcn else 1):
                            out(j)

                if rgcn:
                    turn_tile(1, 0, 0)
                    turn_tile(1, 0, 1)
                    product(1, 0)
                with pe.Fori(0, NST // 2) as pair:
                    x16 = pair * 16 + 16
                    for h in range(2):
                        v, more = rounds_of(pe, sh, bounds, pair * 2 + h)
                        round_(v, h, v + 1, h, pair * 2 + h, x16)
                        with pe.If(more):
                            with pe.Fori(0, more) as i:
                                for k, s in ((1, 1 - h), (2, h)):
                                    u = within(v + i * 2 + k, sh.NR - 3)
                                    round_(u, s, u + 1, h)
                        close(pair * 2 + h, h, x16)
                out(NST)
        clear(nc, sems)


def program(nc, x, src, dst, edge_type, w0, b0, w1, b1, w2, b2, out, dram):
    sh = Shapes(x.shape[0], src.shape[0])
    assert sh.NST % 2 == 0 and sh.N % NB == 0 and sh.NST >= 10
    with ExitStack() as ctx:
        def t(name, shape, dt=FP32):
            return ctx.enter_context(nc.sbuf_tensor(name, shape, dt))

        def landings_of(stage, tiles):
            return [[ctx.enter_context(nc.semaphore(f"{stage}_landed{s}_{c}")) for c in range(tiles)] for s in range(2)]

        res = {
            "iota": t("iota", [P, STRIP]),
            "ident": t("ident", [P, P]),
            "bounds": t("bounds", [P, 2, sh.NST + 1], I32),
            "scales": t("scales", [P, (sh.NST + 2) * NB, 3]),
            "landed": {"s": [ctx.enter_context(nc.semaphore(f"s_landed{k}")) for k in range(2)],
                       "a1": landings_of("a1", SLOTS), "a2": landings_of("a2", SLOTS),
                       "g1": landings_of("g1", NG), "g2": landings_of("g2", NG)},
        }
        build_tables(nc, sh, src, dst, edge_type, dram, res)
        build_coefs(nc, sh, dram, res)
        layer(nc, sh, "a1", True, False, x, x, None, dram["h1"], w0[0], b0[0], dram, res)
        layer(nc, sh, "a2", True, True, dram["h1"], dram["h1"], x, dram["x1"], w0[1], b0[1], dram, res)
        layer(nc, sh, "g1", False, False, dram["x1"], dram["x1"], None, dram["hs"], w1, b1, dram, res)
        layer(nc, sh, "g2", False, True, dram["hs"], dram["hs"], dram["x1"], out, w2, b2, dram, res)


_INS = ["x", "src", "dst", "edge_type_9", "L0_gnn_rgcn_weights", "L0_gnn_rgcn_biases",
        "L1_gnn_W1", "L1_gnn_b1", "L1_gnn_W2", "L1_gnn_b2"]


def kernel(**inputs):
    import numpy as np
    import concourse.bacc as bacc
    from concourse.bass_utils import run_bass_kernel_spmd

    nc = bacc.Bacc("TRN2", target_bir_lowering=False, num_devices=1)
    arrays, args = {}, []
    for name in _INS:
        a = np.ascontiguousarray(inputs[name])
        arrays["in_" + name] = a
        args.append(nc.dram_tensor("in_" + name, a.shape, mybir.dt.from_np(a.dtype), kind="ExternalInput").ap())
    n, e = inputs["x"].shape[0], inputs["src"].shape[0]
    sh = Shapes(n, e)
    dram = {
        "table": nc.dram_tensor("dram_table", (sh.NR * P * SLOTS, WORDS), FP32, kind="Internal").ap(),
        "weights": nc.dram_tensor("dram_weights", (sh.NR * P * SLOTS, 1 + TRI), FP32, kind="Internal").ap(),
        "cbt": nc.dram_tensor("dram_cbt", (sh.NST, KK + 1, STRIP), FP32, kind="Internal").ap(),
        "h1": nc.dram_tensor("dram_h1", (sh.NST * STRIP, D), FP32, kind="Internal").ap(),
        "x1": nc.dram_tensor("dram_x1", (sh.NST * STRIP, D), FP32, kind="Internal").ap(),
        "hs": nc.dram_tensor("dram_hs", (sh.NST * STRIP, D), FP32, kind="Internal").ap(),
    }
    out = nc.dram_tensor("out", (n, D), FP32, kind="ExternalOutput").ap()
    program(nc, *args, out, dram)
    r = run_bass_kernel_spmd(nc, [arrays], core_ids=[0])
    return r.results[0]["out"]
```

```python
import concourse.bass as bass
from concourse import mybir
from contextlib import ExitStack

FP32 = mybir.dt.float32
BF16 = mybir.dt.bfloat16
FP16 = mybir.dt.float16
I32 = mybir.dt.int32
ALU = mybir.AluOpType
ACT = mybir.ActivationFunctionType
AX = mybir.AxisListType

P = 128
D = 128
STRIP = 512
NB = STRIP // P
R = 9
TRI = 3
NG = R // TRI
KK = 2 * R
SLOTS = 2 * NG
WORDS = 5
FILLS = 8
EPS = 1e-5
FAR = 4096


class Shapes:

    def __init__(self, n, e):
        self.N, self.E = n, e
        self.NST = -(-n // STRIP)
        self.LAST = n - (self.NST - 1) * STRIP
        self.COLS = -(-(-(-e // P)) // 14) * 14
        assert self.COLS * P - e < P and self.COLS <= 256
        self.DBINS = self.NST * NG
        self.NR = -(-(2 * self.NST + 2 * e // P + 5) // FILLS) * FILLS
        assert self.NR < 2048


def col(t, i, n=1):
    return t[:, bass.ds(i, n)]


def within(value, most):
    return value.with_bounds(min_val=1, max_val=most)


def rounds_of(eng, sh, bounds, j):
    v = eng.value_load(bounds[0:1, 0, bass.ds(j, 1)], min_val=1, max_val=sh.NR - 2)
    more = eng.value_load(bounds[0:1, 1, bass.ds(j, 1)], min_val=0, max_val=sh.NR // 2)
    return v, more


def each_strip(eng, sh, bounds, first, end, do):
    extra = eng.value_load(bounds[0:1, 1, sh.NST:sh.NST + 1], min_val=0, max_val=sh.NR)
    with eng.If(extra):
        with eng.Fori(first, end) as pair:
            for h in range(2):
                v, more = rounds_of(eng, sh, bounds, pair * 2 + h)
                do(pair, h, v, more)
    with eng.Else():
        with eng.Fori(first, end) as pair:
            for h in range(2):
                do(pair, h, pair * 2 + (h + 1), None)


def further_rounds(eng, sh, v, more, h, do):
    if more is not None:
        with eng.If(more):
            with eng.Fori(0, more) as i:
                do(within(v + i * 2 + 1, sh.NR - 3), 1 - h)
                do(within(v + i * 2 + 2, sh.NR - 3), h)


def last_round(eng, sh, bounds):
    return eng.value_load(bounds[0:1, 0, sh.NST:sh.NST + 1], min_val=sh.NST + 1, max_val=sh.NR - 2)


def landings(v, slot):
    return v * 8 + 8 if slot == 0 else v * 8


def clear(nc, sems):
    with nc.Block() as block:
        @block.sync
        def _(sp):
            for s in sems:
                sp.sem_clear(s)


def build_tables(nc, sh, src, dst, etype, dram, res):
    NST, COLS, DB, NR = sh.NST, sh.COLS, sh.DBINS, sh.NR
    GRP = 7
    GROUPS = COLS // GRP
    full, rest = sh.E // COLS, sh.E % COLS
    iota, ident, bounds = res["iota"], res["ident"], res["bounds"]
    FROWS = NR // FILLS * SLOTS

    sems = []
    with ExitStack() as ctx:
        def t(name, shape, dt=FP32):
            return ctx.enter_context(nc.sbuf_tensor("s_" + name, shape, dt))

        def sem(name):
            sems.append(ctx.enter_context(nc.semaphore("s_" + name)))
            return sems[-1]

        raw = t("raw", [P, 3, COLS], I32)
        ones = t("ones", [P, P], FP16)
        zero = t("zero", [P, 512], FP16)
        before = t("before", [P, P], FP16)
        row0 = t("row0", [P, P], FP16)
        sums = t("sums", [P, 2, 2, DB + 1], FP16)
        ints = t("ints", [P, 4, COLS], I32)
        flts = t("flts", [P, 7, COLS])
        iota16 = t("iota16", [P, DB + 1], FP16)
        key = t("key", [P, 2, COLS])
        slot = t("slot", [P, 2, COLS])
        rec = t("rec", [P, 2, COLS, WORDS])
        onehot = t("onehot", [P, 2, 2, GRP, DB + 1], FP16)
        most = t("most", [P, 3, NST])
        mosti = t("mosti", [P, 2, NST], I32)
        rounds = t("rounds", [P, NST])
        incl = t("incl", [P, NST])
        onesrow = t("onesrow", [P, NST])
        start = t("start", [P, DB + 1], FP16)
        junk = t("junk", [P, 2, 2, DB + 1])
        kst1 = t("kst1", [P, 2, 2, GRP])
        kst = t("kst", [P, 2, 2, GRP])
        posf = t("posf", [P, 2, 2, GRP])
        rows = t("rows", [P, 2, 2, GRP], I32)
        recs = t("recs", [P, 2, 2, GRP, WORDS])
        fill = t("fill", [P, FROWS, WORDS])
        ps_cnt = [ctx.enter_context(nc.psum_tensor(f"s_ps_cnt{d}", [P, 512], FP32)) for d in range(2)]
        ps_pos = [ctx.enter_context(nc.psum_tensor(f"s_ps_pos{d}", [P, 2, 512], FP32)) for d in range(2)]

        raw_cleared, raw_in = sem("raw_cleared"), sem("raw_in")
        consts, fill_ready, filled = sem("consts"), sem("fill_ready"), sem("filled")
        chain, key_ready = sem("chain"), sem("key_ready")
        hot_ready, hist_done = [sem("hot_ready0"), sem("hot_ready1")], [sem("hist_done0"), sem("hist_done1")]
        counted = sem("counted")
        base_ready, hot2_ready = sem("base_ready"), [sem("hot2_ready0"), sem("hot2_ready1")]
        pos_ready, pos_read = [sem("pos_ready0"), sem("pos_ready1")], [sem("pos_read0"), sem("pos_read1")]
        staged, scattered = sem("staged"), res["landed"]["s"]
        sums_ready = [sem("sums_ready0"), sem("sums_ready1")]
        gate, stage_free = sem("gate"), sem("stage_free")
        keys_staged = sem("keys_staged")
        chain2, staged_parts = sem("chain2"), sem("staged_parts")

        def one_hots(d, h, keys):
            for c in range(GRP):
                ins = nc.vector.tensor_scalar(onehot[:, d, h, c, :], iota16[:, :], keys[:, h, d, c:c + 1], None, ALU.is_equal)
            return ins

        with nc.Block() as block:
            @block.sync
            def _(sp):
                sp.wait_ge(raw_cleared, 1)
                for i, a in enumerate((src, dst, etype)):
                    sp.dma_start(raw[0:full, i, :], a[0:full * COLS].rearrange("(p c) -> p c", c=COLS)).then_inc(raw_in, 16)
                    if rest:
                        sp.dma_start(raw[full:full + 1, i, 0:rest],
                                     a[full * COLS:sh.E].rearrange("(p c) -> p c", p=1)).then_inc(raw_in, 16)
                sp.wait_ge(fill_ready, 2)
                table = dram["table"].rearrange("(f p t) w -> f p (t w)", f=FILLS, p=P)
                for f in range(FILLS):
                    sp.dma_start(table[f], fill[:, :, :].rearrange("p t w -> p (t w)")).then_inc(filled, 16)
                for h in range(2):
                    sp.wait_ge(scattered[h], 16 * 2 * GRP * (GROUPS // 2))
                sp.wait_ge(filled, 16 * FILLS)

            @block.gpsimd
            def _(pool):
                nc.gpsimd.memset(before[:, :], 1.0).then_inc(consts, 1)
                nc.gpsimd.memset(row0[:, :], float(P)).then_inc(consts, 1)
                nc.gpsimd.memset(ident[:, :], 0.0).then_inc(consts, 1)
                nc.gpsimd.iota(iota[:, :], pattern=[[1, STRIP]], base=0, channel_multiplier=0,
                               allow_small_or_imprecise_dtypes=True).then_inc(consts, 1)
                nc.gpsimd.memset(fill[:, :, :], -1.0).then_inc(consts, 1)
                pool.wait_ge(consts, 5)
                nc.gpsimd.affine_select(out=before[:, :], in_=before[:, :], compare_op=ALU.is_gt, fill=0.0, base=0,
                                        pattern=[[1, P]], channel_multiplier=-1).then_inc(consts, 1)
                nc.gpsimd.affine_select(out=row0[:, :], in_=row0[:, :], compare_op=ALU.is_equal, fill=0.0, base=0,
                                        pattern=[[0, P]], channel_multiplier=1).then_inc(consts, 1)
                nc.gpsimd.affine_select(out=ident[:, :], in_=ident[:, :], compare_op=ALU.not_equal, fill=1.0, base=0,
                                        pattern=[[1, P]], channel_multiplier=-1).then_inc(consts, 1)
                nc.gpsimd.memset(fill[:, :, 0:1], 0.0).then_inc(fill_ready, 2)
                pool.wait_ge(filled, 16 * FILLS)
                with pool.Fori(0, GROUPS // 2) as i:
                    for h in range(2):
                        pool.wait_ge(staged, i * 2 + (h + 1))
                        pool.sem_inc(gate, 1)
                        for d in range(2):
                            for c in range(GRP):
                                nc.gpsimd.indirect_dma_start(
                                    dram["table"], bass.IndirectOffsetOnAxis(ap=rows[:, h, d, c:c + 1], axis=0),
                                    recs[:, h, d, c, :], None).then_inc(scattered[h], 16)
                    for h in range(2):
                        pool.wait_ge(scattered[h], (i + 1) * (16 * 2 * GRP))
                        pool.sem_inc(stage_free, 1)

            @block.vector
            def _(v):
                n = [0]

                def link(ins):
                    n[0] += 1
                    ins.then_inc(chain, 1)
                    v.wait_ge(chain, n[0])

                V = nc.vector
                V.memset(zero[:, :], 0.0)
                V.memset(ones[:, :], 1.0)
                V.memset(sums[:, :, 0, :], 0.0)
                V.memset(onesrow[:, :], 1.0)
                link(V.memset(raw[:, 0:2, :], NST * STRIP))
                V.memset(raw[:, 2, :], 0).then_inc(raw_cleared, 1)
                v.wait_ge(raw_in, 48 * (2 if rest else 1))
                v.wait_ge(consts, 8)
                V.tensor_copy(iota16[:, :], iota[:, 0:DB + 1])
                ty, tg, rel3, a, b, pad, stf = (flts[:, k, :] for k in range(7))
                strip, loc, blk, pp = (ints[:, k, :] for k in range(4))
                link(V.tensor_copy(ty, raw[:, 2, :]))
                link(V.tensor_scalar(a, ty, float(TRI), None, ALU.is_ge))
                link(V.tensor_scalar(b, ty, float(2 * TRI), None, ALU.is_ge))
                link(V.tensor_tensor(tg, a, b, ALU.add))
                link(V.scalar_tensor_tensor(rel3, tg, -float(TRI), ty, ALU.mult, ALU.add))
                for d in range(2):
                    link(V.tensor_scalar(strip, raw[:, d, :], STRIP.bit_length() - 1, None, ALU.logical_shift_right))
                    link(V.tensor_copy(stf, strip))
                    link(V.scalar_tensor_tensor(key[:, d, :], stf, float(NG), tg, ALU.mult, ALU.add))
                v.sem_inc(key_ready, 1)

                with v.Fori(0, GROUPS // 2) as i:
                    for h in range(2):
                        g = i * 2 + h
                        V.tensor_copy(kst1[:, h, :, :], key[:, :, bass.ds(g * GRP, GRP)]).then_inc(keys_staged, 1)
                        v.wait_ge(keys_staged, g + 1)
                        for d in range(2):
                            v.wait_ge(hist_done[d], g + 1)
                            one_hots(d, h, kst1).then_inc(hot_ready[d], 1)
                for d in range(2):
                    node, other = raw[:, d, :], raw[:, 1 - d, :]
                    link(V.tensor_scalar(strip, node, STRIP.bit_length() - 1, None, ALU.logical_shift_right))
                    link(V.tensor_scalar(loc, node, STRIP - 1, None, ALU.bitwise_and))
                    link(V.tensor_scalar(blk, loc, NB - 1, None, ALU.bitwise_and))
                    link(V.tensor_scalar(pp, loc, NB.bit_length() - 1, None, ALU.logical_shift_right))
                    link(V.tensor_copy(stf, strip))
                    link(V.tensor_scalar(slot[:, d, :], tg, float(d * NG), None, ALU.add))
                    link(V.tensor_scalar(pad, stf, float(NST), -float(FAR), ALU.is_ge, ALU.mult))
                    link(V.tensor_scalar(rec[:, d, :, 0].bitcast(I32), other, float(sh.N - 1), None, ALU.min))
                    link(V.scalar_tensor_tensor(a, blk, float(P), pp, ALU.mult, ALU.add))
                    link(V.tensor_tensor(rec[:, d, :, 1], a, pad, ALU.add))
                    link(V.scalar_tensor_tensor(a, blk, float(KK), pad, ALU.mult, ALU.add))
                    link(V.scalar_tensor_tensor(b, ty, 2.0, a, ALU.mult, ALU.add))
                    link(V.tensor_scalar(rec[:, d, :, 2], b, float(d), None, ALU.add))
                    link(V.tensor_copy(rec[:, d, :, 3], rel3))
                    link(V.tensor_tensor(rec[:, d, :, 4], pp, pad, ALU.add))
                v.wait_ge(counted, 1)
                for d in range(2):
                    link(V.tensor_reduce(most[:, d, :], ps_cnt[d][:, 0:DB].rearrange("p (s g) -> p s g", g=NG),
                                         AX.X, ALU.max))
                link(V.tensor_tensor(most[:, 2, :], most[:, 0, :], most[:, 1, :], ALU.max))
                link(V.tensor_scalar(mosti[:, 0, :], most[:, 2, :], float(P - 1), None, ALU.add))
                link(V.tensor_scalar(mosti[:, 1, :], mosti[:, 0, :], 8, None, ALU.logical_shift_right))
                link(V.tensor_copy(bounds[:, 1, 0:NST], mosti[:, 1, :]))
                link(V.tensor_scalar(rounds[:, :], mosti[:, 1, :], 2.0, 1.0, ALU.mult, ALU.add))
                link(V.tensor_tensor_scan(incl[:, :], onesrow[:, :], rounds[:, :], 1.0, ALU.mult, ALU.add))
                link(V.tensor_tensor(most[:, 0, :], incl[:, :], rounds[:, :], ALU.subtract))
                link(V.tensor_copy(bounds[:, 0, 0:NST], most[:, 0, :]))
                link(V.tensor_copy(bounds[:, 0, NST:NST + 1], incl[:, NST - 1:NST]))
                link(V.tensor_scalar(bounds[:, 1, NST:NST + 1], incl[:, NST - 1:NST], -float(NST + 1), None, ALU.add))
                link(V.tensor_copy(start[:, 0:DB].rearrange("p (s g) -> p s g", g=NG),
                                   most[:, 0, :].unsqueeze(2).to_broadcast([P, NST, NG])))
                link(V.tensor_copy(start[:, DB:DB + 1], incl[:, NST - 1:NST]))
                v.sem_inc(base_ready, 1)

                with v.Fori(0, GROUPS // 2) as i:
                    for h in range(2):
                        g = i * 2 + h
                        V.tensor_copy(kst[:, h, :, :], key[:, :, bass.ds(g * GRP, GRP)]).then_inc(chain2, 1)
                        v.wait_ge(chain2, g + 1)
                        for d in range(2):
                            v.wait_ge(pos_ready[d], g * GRP + 1)
                            one_hots(d, h, kst).then_inc(hot2_ready[d], 1)
                        for c in range(GRP):
                            at = g * GRP + (c + 2)
                            for d in range(2):
                                v.wait_ge(pos_ready[d], at)
                                was, now = (h * GRP + c) % 2, (h * GRP + c + 1) % 2
                                V.tensor_tensor(sums[:, d, now, :], sums[:, d, was, :], onehot[:, d, h, c, :], ALU.add) \
                                    .then_inc(sums_ready[d], 1)
                                V.scalar_tensor_tensor(junk[:, d, was, :], iota[:, 0:DB + 1], kst[:, h, d, c:c + 1],
                                                       ps_pos[d][:, was, 0:DB + 1], ALU.is_equal, ALU.mult,
                                                       accum_out=posf[:, h, d, c:c + 1]).then_inc(pos_read[d], 1)
                        for d in range(2):
                            v.wait_ge(pos_read[d], g * GRP + (GRP + 2))
                        v.wait_ge(stage_free, g + 1)
                        V.scalar_tensor_tensor(rows[:, h, :, :], posf[:, h, :, :], float(SLOTS),
                                               slot[:, :, bass.ds(g * GRP, GRP)], ALU.mult, ALU.add).then_inc(staged_parts, 1)
                        V.tensor_copy(recs[:, h, :, :, :], rec[:, :, bass.ds(g * GRP, GRP), :]).then_inc(staged_parts, 1)
                        v.wait_ge(staged_parts, g * 2 + 2)
                        v.sem_inc(staged, 1)

            @block.scalar
            def _(act):
                for d in range(2):
                    act.sem_inc(hist_done[d], 2)
                    act.sem_inc(pos_ready[d], 1)
                    act.sem_inc(pos_read[d], 2)
                    act.sem_inc(sums_ready[d], 1)
                act.sem_inc(stage_free, 2)

            @block.tensor
            def _(pe):
                pe.wait_ge(consts, 8)
                T = nc.tensor
                pe.wait_ge(key_ready, 1)
                for d in range(2):
                    T.matmul(ps_cnt[d][:, 0:DB + 1], zero[:, 0:P], zero[:, 0:DB + 1], start=True, stop=False)
                with pe.Fori(0, GROUPS // 2) as i:
                    for h in range(2):
                        for d in range(2):
                            pe.wait_ge(hot_ready[d], i * 2 + (h + 1))
                            for c in range(GRP):
                                ins = T.matmul(ps_cnt[d][:, 0:DB + 1], ones[:, :], onehot[:, d, h, c, :],
                                               start=False, stop=False)
                            ins.then_inc(hist_done[d], 1)
                for d in range(2):
                    ins = T.matmul(ps_cnt[d][:, 0:DB + 1], zero[:, 0:P], zero[:, 0:DB + 1], start=False, stop=True)
                ins.then_inc(counted, 1)
                pe.wait_ge(base_ready, 1)
                with pe.Fori(0, GROUPS // 2) as i:
                    for h in range(2):
                        g = i * 2 + h
                        for d in range(2):
                            pe.wait_ge(hot2_ready[d], g + 1)
                        for c in range(GRP):
                            at = g * GRP + (c + 1)
                            for d in range(2):
                                out = ps_pos[d][:, (h * GRP + c) % 2, 0:DB + 1]
                                pe.wait_ge(pos_read[d], at)
                                T.matmul(out, row0[:, :], start[:, :], start=True, stop=False)
                                T.matmul(out, before[:, :], onehot[:, d, h, c, :], start=False, stop=False)
                                pe.wait_ge(sums_ready[d], at)
                                T.matmul(out, ones[:, :], sums[:, d, (h * GRP + c) % 2, :],
                                         start=False, stop=True).then_inc(pos_ready[d], 1)
        clear(nc, sems)


def build_coefs(nc, sh, dram, res):
    NST = sh.NST
    NBLK = NST * NB
    W = NB * KK
    iota, ident, bounds = res["iota"], res["ident"], res["bounds"]
    cself = res["scales"][:, 0:NBLK, 0]
    sdeg, dinv = (res["scales"][:, 2 * NB:2 * NB + NBLK, k] for k in (1, 2))

    sems = []
    with ExitStack() as ctx:
        def t(name, shape, dt=FP32):
            return ctx.enter_context(nc.sbuf_tensor("c_" + name, shape, dt))

        def sem(name):
            sems.append(ctx.enter_context(nc.semaphore("c_" + name)))
            return sems[-1]

        rec = t("rec", [P, 2, SLOTS, WORDS])
        rec2 = t("rec2", [P, 2, SLOTS, WORDS])
        rec3 = t("rec3", [P, 2, SLOTS, WORDS])
        spare = t("spare", [P, SLOTS, WORDS])
        zero = t("zero", [P, P], BF16)
        identb = t("identb", [P, P], BF16)
        hot_p = t("hot_p", [P, 2, SLOTS, P], BF16)
        hot_w = t("hot_w", [P, 2, SLOTS, W], BF16)
        hot_t = t("hot_t", [P, SLOTS, P], BF16)
        cnt = t("cnt", [P, NBLK, KK])
        pa = t("pa", [P, NBLK, KK])
        pb = t("pb", [P, NBLK, KK])
        pb3 = t("pb3", [P, 3, NBLK, KK], BF16)
        deg = t("deg", [P, NBLK])
        stage = t("stage", [P, 2, NB, KK + 1])
        cbt = t("cbt", [KK + 1, 2, STRIP])
        junk = t("junk", [P, 2, SLOTS, W])
        coef = t("coef", [P, 2, SLOTS])
        wts = t("wts", [P, 2, SLOTS, 1 + TRI])
        ps_cnt = ctx.enter_context(nc.psum_tensor("c_ps_cnt", [P, 2, 512], FP32))
        ps_t = ctx.enter_context(nc.psum_tensor("c_ps_t", [P, 1024], BF16))
        ps_q = ctx.enter_context(nc.psum_tensor("c_ps_q", [P, 2, 512], FP32))

        chain, consts = sem("chain"), sem("consts")
        carried = sem("carried")
        rec_land, rec2_land, rec3_land = ([sem(f"{r}_land{s}") for s in range(2)] for r in ("rec", "rec2", "rec3"))
        hot_ready, round_mm, closed, cnt_out = sem("hot_ready"), sem("round_mm"), sem("closed"), sem("cnt_out")
        coefs_ready, staged, cb_ps, cb_sb = sem("coefs_ready"), sem("staged"), sem("cb_ps"), sem("cb_sb")
        cb_free, cb_out = sem("cb_free"), [sem("cb_out0"), sem("cb_out1")]
        hp_ready, hp_ps, hp_sb = sem("hp_ready"), sem("hp_ps"), sem("hp_sb")
        q_ps, q_read, wts_ready = sem("q_ps"), sem("q_read"), sem("wts_ready")
        wts_land, wts_free = [sem("wts_land0"), sem("wts_land1")], sem("wts_free")

        table = dram["table"].rearrange("(v p c) w -> v p (c w)", p=P, c=SLOTS)
        weights = dram["weights"].rearrange("(v p c) w -> v p (c w)", p=P, c=SLOTS)

        def row(eng, r, land, v, s):
            eng.dma_start(r[:, s, :, :].rearrange("p c w -> p (c w)"), one(table, v)).then_inc(land[s], 16)

        def one(a, v):
            return a[bass.ds(v, 1), :, :].rearrange("v p n -> (v p) n")

        def one_hot(out, r, s, word, width):
            numbers = iota[:, 0:width].unsqueeze(1).to_broadcast([P, SLOTS, width])
            return nc.vector.tensor_tensor(out, numbers, r[:, s, :, word].unsqueeze(2).to_broadcast([P, SLOTS, width]),
                                           ALU.is_equal)

        def every_round(eng, body):
            def strip(pair, h, v, more):
                j = pair * 2 + h
                body(v, h, j, h, True)
                further_rounds(eng, sh, v, more, h, lambda u, s: body(u, s, j, h, False))

            each_strip(eng, sh, bounds, 0, NST // 2, strip)

        with nc.Block() as block:
            @block.sync
            def _(sp):
                sp.dma_start(spare[:, :, :].rearrange("p c w -> p (c w)"), one(table, 1)).then_inc(wts_land[1], 16)
                for v in (1, 2):
                    row(sp, rec, rec_land, v, v - 1)
                    row(sp, rec2, rec2_land, v, v - 1)
                    row(sp, rec3, rec3_land, v, v - 1)

                def counting(v, s, j, h, main):
                    sp.wait_ge(hot_ready, v)
                    sp.sem_inc(carried, 1)
                    row(sp, rec, rec_land, within(v + 2, sh.NR - 1), s)

                every_round(sp, counting)
                def weighing(v, s, j, h, main, first=False):
                    sp.wait_ge(wts_ready, v)
                    sp.sem_inc(carried, 1)
                    sp.dma_start(one(weights, v), wts[:, s, :, :].rearrange("p c w -> p (c w)")).then_inc(wts_land[s], 16)
                    row(sp, rec2, rec2_land, within(v + 2, sh.NR - 1), s)
                    if main:
                        sp.wait_ge(cb_sb, j + 3)
                        sp.sem_inc(carried, 1)
                        sp.dma_start(dram["cbt"][bass.ds(j, 1), :, :].rearrange("s k n -> (s k) n"),
                                     cbt[:, h, :]).then_inc(cb_out[h], 16)
                    sp.wait_ge(wts_land[1 - s], landings(v, s))
                    sp.sem_inc(wts_free, 1)
                    if main and not first:
                        sp.wait_ge(cb_out[1 - h], (j - 1 - (1 - h)) * 8 + 16)
                        sp.sem_inc(cb_free, 1)

                def strip(pair, h, v, more):
                    j = pair * 2 + h
                    weighing(v, h, j, h, True, isinstance(j, int) and j == 0)
                    further_rounds(sp, sh, v, more, h, lambda u, s: weighing(u, s, j, h, False))

                for h in range(2):
                    strip(0, h, *rounds_of(sp, sh, bounds, h))
                each_strip(sp, sh, bounds, 1, NST // 2, strip)
                end = last_round(sp, sh, bounds)
                sp.wait_ge(cb_out[1], (NST // 2) * 16)
                sp.wait_ge(cb_out[0], (NST // 2) * 16)
                for k in range(2):
                    sp.dma_start(one(weights, within(end + k, sh.NR - 1)),
                                 wts[:, k, :, :].rearrange("p c w -> p (c w)")).then_inc(wts_land[k], 16)
                for k in range(2):
                    sp.wait_ge(wts_land[k], landings(end + k, k) + 16 * k)
                    sp.wait_ge(rec_land[k], landings(end + k, k))
                    sp.wait_ge(rec2_land[k], landings(end + k, k))
                    sp.wait_ge(rec3_land[k], landings(end + 2 - k, k))
                    sp.sem_inc(carried, 1)

            @block.vector
            def _(v_):
                n = [0]
                V = nc.vector

                def link(ins):
                    n[0] += 1
                    ins.then_inc(chain, 1)
                    v_.wait_ge(chain, n[0])

                V.memset(res["scales"][:, :, 0:1], 0.0)
                V.memset(res["scales"][:, :, 1:3], 1.0)
                V.memset(zero[:, :], 0.0)
                link(V.tensor_copy(identb[:, :], ident[:, :]))
                v_.sem_inc(consts, 1)

                def counting(v, s, j, h, main):
                    v_.wait_ge(rec_land[s], landings(v, s))
                    v_.wait_ge(round_mm, v)
                    one_hot(hot_p[:, s, :, :], rec, s, 4, P)
                    one_hot(hot_w[:, s, :, :], rec, s, 2, W).then_inc(hot_ready, 1)

                every_round(v_, counting)
                v_.wait_ge(cnt_out, NST + 2)
                link(V.tensor_scalar(pa[:, :, :], cnt[:, :, :], 1.0, None, ALU.max))
                link(V.reciprocal(pb[:, :, :], pa[:, :, :]))
                link(V.tensor_scalar(pa[:, :, :], pb[:, :, :], 2.0, None, ALU.mult))
                a, b = pa, pb
                s = 1
                while s < KK:
                    V.tensor_tensor(b[:, :, 0:KK - s], a[:, :, 0:KK - s], a[:, :, s:KK], ALU.mult)
                    link(V.tensor_copy(b[:, :, KK - s:KK], a[:, :, KK - s:KK]))
                    a, b = b, a
                    s *= 2
                assert a is pb
                link(V.tensor_copy(cself, pb[:, :, 0]))
                link(V.tensor_reduce(deg[:, :], cnt[:, :, :].rearrange("p b (r d) -> p b d r", d=2)[:, :, 1, :],
                                     AX.X, ALU.add))
                link(V.tensor_scalar(deg[:, :], deg[:, :], 1.0, None, ALU.add))
                v_.sem_inc(coefs_ready, 1)
                v_.wait_ge(coefs_ready, 2)
                link(V.reciprocal(dinv, sdeg))
                link(V.tensor_tensor(pa[:, :, :], cnt[:, :, :], pb[:, :, :], ALU.mult))
                link(V.tensor_copy(pb3[:, 0, :, :], pb[:, :, :]))
                link(V.tensor_tensor(cnt[:, :, :], pb[:, :, :], pb3[:, 0, :, :], ALU.subtract))
                link(V.tensor_copy(pb3[:, 1, :, :], cnt[:, :, :]))
                link(V.tensor_tensor(cnt[:, :, :], cnt[:, :, :], pb3[:, 1, :, :], ALU.subtract))
                link(V.tensor_copy(pb3[:, 2, :, :], cnt[:, :, :]))

                def turned(v, s):
                    v_.wait_ge(rec3_land[s], landings(v, s))
                    one_hot(hot_p[:, s, :, :], rec3, s, 4, P).then_inc(hp_ready, 1)

                def weighing(v, s, j, h, main):
                    turned(within(v + 1, sh.NR - 2), 1 - s)
                    if main:
                        v_.wait_ge(cb_ps, j + 1)
                        V.tensor_copy(stage[:, h, :, 0:KK], pa[:, bass.ds(j * NB, NB), :])
                        V.tensor_copy(stage[:, h, :, KK:KK + 1], pb[:, bass.ds(j * NB, NB), 0:1]).then_inc(staged, 1)
                    v_.wait_ge(rec2_land[s], landings(v, s))
                    v_.wait_ge(q_ps, v)
                    for c in range(SLOTS):
                        V.scalar_tensor_tensor(junk[:, s, c, :], iota[:, 0:W], rec2[:, s, c, 2:3],
                                               ps_q[:, s, c * W:c * W + W], ALU.is_equal, ALU.mult,
                                               accum_out=coef[:, s, c:c + 1]).then_inc(q_read, 1)
                    v_.wait_ge(wts_free, v)
                    V.tensor_copy(wts[:, s, :, 0], rec2[:, s, :, 1])
                    v_.wait_ge(q_read, v * SLOTS)
                    for i in range(TRI):
                        ins = V.scalar_tensor_tensor(wts[:, s, :, 1 + i], rec2[:, s, :, 3], float(i), coef[:, s, :],
                                                     ALU.is_equal, ALU.mult)
                    ins.then_inc(wts_ready, 1)

                turned(1, 0)
                every_round(v_, weighing)

            @block.scalar
            def _(act):
                act.sem_inc(round_mm, 2)
                act.sem_inc(cnt_out, 2)
                act.sem_inc(cb_ps, 2)
                act.sem_inc(cb_sb, 2)
                act.sem_inc(cb_free, 2)
                act.sem_inc(wts_free, 1)
                C = nc.scalar
                with act.Fori(0, NST // 2) as pair:
                    for h in range(2):
                        j = pair * 2 + h
                        act.wait_ge(closed, j + 1)
                        C.activation(cnt[:, bass.ds(j * NB, NB), :].rearrange("p b k -> p (b k)"),
                                     ps_cnt[:, h, 0:W], ACT.Copy).then_inc(cnt_out, 1)
                act.wait_ge(coefs_ready, 1)
                C.activation(sdeg, deg[:, :], ACT.Sqrt).then_inc(coefs_ready, 1)
                def turned_copy(v):
                    act.wait_ge(hp_ps, v)
                    C.activation(hot_t[:, :, :].rearrange("p k m -> p (k m)"), ps_t[:, 0:SLOTS * P], ACT.Copy) \
                        .then_inc(hp_sb, 1)

                def weighing(v, s, j, h, main):
                    turned_copy(v + 1)
                    row(act, rec3, rec3_land, within(v + 3, sh.NR - 1), 1 - s)
                    if main:
                        act.wait_ge(cb_ps, j + 3)
                        act.wait_ge(cb_free, j + 1)
                        C.activation(cbt[:, h, :], ps_cnt[0:KK + 1, h, :], ACT.Copy).then_inc(cb_sb, 1)

                turned_copy(1)
                row(act, rec3, rec3_land, 3, 0)
                every_round(act, weighing)

            @block.tensor
            def _(pe):
                M = nc.tensor
                pe.wait_ge(consts, 1)

                def counting(v, s, j, h, main):
                    if main:
                        pe.wait_ge(cnt_out, j + 1)
                    pe.wait_ge(hot_ready, v)
                    for c in range(SLOTS):
                        ins = M.matmul(ps_cnt[:, h, 0:W], hot_p[:, s, c, :], hot_w[:, s, c, :],
                                       start=main and c == 0, stop=False)
                    ins.then_inc(round_mm, 1)

                def strip(pair, h, v, more):
                    j = pair * 2 + h
                    counting(v, h, j, h, True)
                    further_rounds(pe, sh, v, more, h, lambda u, s: counting(u, s, j, h, False))
                    M.matmul(ps_cnt[:, h, 0:W], zero[:, :], zero[:, 0:W], start=False, stop=True).then_inc(closed, 1)

                each_strip(pe, sh, bounds, 0, NST // 2, strip)
                def turn(v, s):
                    pe.wait_ge(hp_ready, v)
                    for c in range(SLOTS):
                        ins = M.transpose(ps_t[:, c * P:c * P + P], hot_p[:, s, c, :], identb[:, :])
                    ins.then_inc(hp_ps, 1)

                def weighing(v, s, j, h, main):
                    pe.wait_ge(hp_sb, v)
                    for c in range(SLOTS):
                        for k in range(3):
                            ins = M.matmul(ps_q[:, s, c * W:c * W + W], hot_t[:, c, :],
                                           pb3[:, k, bass.ds(j * NB, NB), :].rearrange("p b k -> p (b k)"),
                                           start=k == 0, stop=k == 2)
                    ins.then_inc(q_ps, 1)
                    turn(v + 1, 1 - s)
                    if main:
                        pe.wait_ge(staged, j + 1)
                        pe.wait_ge(cb_sb, j + 1)
                        for b in range(NB):
                            ins = M.transpose(ps_cnt[0:KK + 1, h, b * P:b * P + P], stage[:, h, b, :], ident[:, :])
                        ins.then_inc(cb_ps, 1)

                turn(1, 0)
                every_round(pe, weighing)
        clear(nc, sems)


def layer(nc, sh, name, rgcn, last, gathered, own, residual, to, weights, bias, dram, res):
    NST = sh.NST
    iota, ident, bounds, scales = res["iota"], res["ident"], res["bounds"], res["scales"]
    S = SLOTS if rgcn else NG
    C0 = SLOTS - S
    SB = 1 if rgcn else 2
    late = last and not rgcn
    CONSTS = 9

    sems = []
    with ExitStack() as ctx:
        def t(n_, shape, dt=FP32):
            return ctx.enter_context(nc.sbuf_tensor(f"{name}_{n_}", shape, dt))

        def ps(n_, shape):
            return ctx.enter_context(nc.psum_tensor(f"{name}_{n_}", shape, FP32))

        def sem(n_):
            sems.append(ctx.enter_context(nc.semaphore(f"{name}_{n_}")))
            return sems[-1]

        def sems_of(n_, count):
            return [sem(f"{n_}{k}") for k in range(count)]

        rec = t("rec", [P, 2, SLOTS, WORDS])
        wts = t("wts", [P, 2, SLOTS, 1 + TRI])
        xg = t("xg", [P, 2, S, D])
        xin = t("xin", [P, 2, STRIP])
        xres = t("xres", [P, 2, STRIP])
        sc = t("sc", [P, 2, NB, 3])
        ht = t("ht", [D, STRIP])
        sel = t("sel", [P, SB, S, STRIP])
        outb = t("outb", [P, 2, STRIP])
        eps = t("eps", [P, 1])
        if rgcn:
            xc = t("xc", [P, STRIP])
            xt = t("xt", [D, STRIP])
            wall = t("wall", [D, KK * D])
            wself = t("wself", [D, D])
            ball = t("ball", [KK + 1, D])
            cb = t("cb", [KK + 1, 2, STRIP])
            turned = t("turned", [P, S, P])
            part = t("part", [P, S, D])
            mid = t("mid", [P, S, D])
            y = t("y", [P, S, D])
            ps_xt = ps("ps_xt", [P, 2, 512])
            ps_y = ps("ps_y", [P, 2, 512])
        else:
            wgcn = t("wgcn", [D, D])
            brow = t("brow", [P, D])
        z = t("z", [P, 2, STRIP])
        if last:
            stats = t("stats", [P, NB, 6])
            mv = t("mv", [P, NB, 2])
            sd = t("sd", [P, NB])
            rs = t("rs", [P, NB])
            rs2 = t("rs2", [P, NB])
            shift = t("shift", [P, NB])
        if not rgcn:
            za = t("za", [P, STRIP])
            zb = t("zb", [P, STRIP])
        ps_h = ps("ps_h", [P, 2, STRIP])
        ps_x = ps("ps_x", [P, STRIP]) if rgcn else None
        ps_o = ps("ps_o", [P, STRIP])

        landed = res["landed"][name]
        w_in, consts, gate = sem("w_in"), sem("consts"), sem("gate")
        carried = sem("carried")
        rec_land, wts_land = sems_of("rec_land", 2), sems_of("wts_land", 2)
        sel_sb, used = sems_of("sel_sb", S), sems_of("used", S)
        if rgcn:
            xt_ps, xt_sb = sems_of("xt_ps", S), sems_of("xt_sb", S)
            y_ps, part_sb, mid_sb, y_sb = (sems_of(n_, S) for n_ in ("y_ps", "part_sb", "mid_sb", "y_sb"))
            cb_land, xc_sb = sems_of("cb_land", 2), sem("xc_sb")
        in_land, res_land, st_land = sems_of("in_land", 2), sems_of("res_land", 2), sems_of("st_land", 2)
        closed = sem("closed")
        sc_sb, own_ps, own_sb = sem("sc_sb"), sem("own_ps"), sem("own_sb")
        ht_sb, out_ps, out_read = sem("ht_sb"), sem("out_ps"), sem("out_read")
        res_ready, res_read, out_free = sem("res_ready"), sem("res_read"), sem("out_free")
        fin, relu_sb = sem("fin"), sem("relu_sb")
        passed, var_ready, sd_ready = sem("passed"), sem("var_ready"), sem("sd_ready")
        fin_links = sems_of("fin_link", 6)

        def strip_rows(a, j, n_rows=STRIP):
            start = j * STRIP
            rows = a[start:start + n_rows, :] if isinstance(j, int) else a[bass.ds(start, n_rows), :]
            return rows.rearrange("(p b) d -> p (b d)", b=NB)

        def strip_parts(j):
            return sh.LAST // NB if isinstance(j, int) and j == NST - 1 else P

        with nc.Block() as block:
            @block.gpsimd
            def _(pool):
                def gather(v, s, c):
                    pool.wait_ge(used[c], v)
                    pool.sem_inc(gate, 1)
                    nc.gpsimd.indirect_dma_start(
                        xg[:, s, c, :], None, gathered[0:sh.N, :],
                        bass.IndirectOffsetOnAxis(ap=rec[:, s, C0 + c, 0:1].bitcast(I32), axis=0)) \
                        .then_inc(landed[s][c], 16)

                def round_(v, s):
                    pool.wait_ge(rec_land[s], landings(v, s))
                    for c in range(S):
                        gather(v, s, c)

                def strip(pair, h, v, more):
                    round_(v, h)
                    further_rounds(pool, sh, v, more, h, round_)

                each_strip(pool, sh, bounds, 0, NST // 2, strip)
                if rgcn:
                    end = last_round(pool, sh, bounds)
                    pool.wait_ge(rec_land[0], landings(end, 0))
                    for c in range(2):
                        gather(end, 0, c)

            @block.sync
            def _(sp):
                def first_loads():
                    for k in range(2):
                        load_rec(k + 1, k)
                        load_wts(k + 1, k)

                def load_weights():
                    if not rgcn:
                        sp.dma_start(wgcn[:, :], weights).then_inc(w_in, 16)
                        sp.dma_start(brow[:, :], bias.rearrange("(o d) -> o d", o=1).to_broadcast([P, D])).then_inc(w_in, 16)
                        return
                    for d in range(2):
                        sp.dma_start(wall[:, d * R * D:(d + 1) * R * D].rearrange("k (r m) -> k r m", m=D),
                                     weights[d * R:(d + 1) * R, :, :].rearrange("r k m -> k r m")).then_inc(w_in, 16)
                        sp.dma_start(ball[d:KK:2, :], bias[d * R:(d + 1) * R, :]).then_inc(w_in, 16)
                    sp.dma_start(wself[:, :], weights[KK, :, :]).then_inc(w_in, 16)
                    sp.dma_start(ball[KK:KK + 1, :], bias[KK:KK + 1, :]).then_inc(w_in, 16)

                def table_row(a, v):
                    rows = dram[a].rearrange("(v p c) w -> v p (c w)", p=P, c=SLOTS)
                    return rows[bass.ds(v, 1), :, :].rearrange("v p n -> (v p) n")

                def load_rec(v, s):
                    sp.dma_start(rec[:, s, :, :].rearrange("p c w -> p (c w)"), table_row("table", v)) \
                        .then_inc(rec_land[s], 16)

                def load_wts(v, s):
                    sp.dma_start(wts[:, s, :, :].rearrange("p c w -> p (c w)"), table_row("weights", v)) \
                        .then_inc(wts_land[s], 16)

                def load_own(j, h):
                    sp.dma_start(xin[0:strip_parts(j), h, :], strip_rows(own, j, strip_parts(j) * NB)).then_inc(in_land[h], 16)

                def load_cb(j, h):
                    sp.dma_start(cb[:, h, :], dram["cbt"][bass.ds(j, 1), :, :].rearrange("s k n -> (s k) n")) \
                        .then_inc(cb_land[h], 16)

                def load_res(j, h):
                    sp.dma_start(xres[0:strip_parts(j), h, :], strip_rows(residual, j, strip_parts(j) * NB)) \
                        .then_inc(res_land[h], 16)

                def rec_ahead(v, s):
                    for c in range(S):
                        sp.wait_ge(landed[s][c], landings(v, s))
                    sp.sem_inc(carried, 1)
                    load_rec(within(v + 2, sh.NR - 1), s)

                def wts_ahead(v, s):
                    sp.wait_ge(used[S - 1], v + 2)
                    sp.sem_inc(carried, 1)
                    load_wts(within(v + 2, sh.NR - 1), s)

                def strip_dmas(j, h):
                    if rgcn and (not isinstance(j, int) or j + 2 < NST):
                        sp.wait_ge(xc_sb, j + 1)
                        sp.sem_inc(carried, 1)
                        load_own(j + 2, h)
                    if not isinstance(j, int) or 1 <= j < NST - 1:
                        sp.wait_ge(closed, j + 1)
                        sp.sem_inc(carried, 1)
                        if rgcn:
                            load_cb(j + 1, 1 - h)
                        else:
                            load_own(j + 1, 1 - h)
                    if last and (not isinstance(j, int) or 1 <= j <= NST):
                        sp.wait_ge(res_read, j)
                        sp.sem_inc(carried, 1)
                        load_res(j - 1, 1 - h)
                    if not isinstance(j, int) or 3 <= j:
                        k = j - 3
                        sp.wait_ge(fin, k + 5)
                        sp.sem_inc(carried, 1)
                        sp.dma_start(strip_rows(to, k, strip_parts(k) * NB), outb[0:strip_parts(k), 1 - h, :]) \
                            .then_inc(st_land[1 - h], 16)

                def relay(j, h):
                    if last and (not isinstance(j, int) or 1 <= j <= NST):
                        sp.wait_ge(res_land[1 - h], (j - 1 - (1 - h)) * 8 + 16)
                        sp.sem_inc(res_ready, 1)
                    if not isinstance(j, int) or j >= 3:
                        sp.wait_ge(st_land[1 - h], (j - 3 - (1 - h)) * 8 + 16)
                        sp.sem_inc(out_free, 1)

                def step(pair, h, v, more):
                    j = pair * 2 + h
                    relay(j - 1, 1 - h)
                    rec_ahead(v, h)
                    strip_dmas(j, h)
                    wts_ahead(v, h)

                    def both_ahead(u, s):
                        rec_ahead(u, s)
                        wts_ahead(u, s)

                    further_rounds(sp, sh, v, more, h, both_ahead)

                first_loads()
                load_weights()
                sp.wait_ge(consts, CONSTS)
                for k in range(2):
                    load_own(k, k)
                    if rgcn:
                        load_cb(k, k)
                for j in range(4):
                    step(j // 2, j % 2, *rounds_of(sp, sh, bounds, j))
                each_strip(sp, sh, bounds, 2, (NST - 4) // 2, step)
                for j in range(NST - 4, NST):
                    step(j // 2, j % 2, *rounds_of(sp, sh, bounds, j))
                for j in range(NST, NST + 3):
                    relay(j - 1, 1 - j % 2)
                    strip_dmas(j, j % 2)
                relay(NST + 2, NST % 2)
                end = last_round(sp, sh, bounds)
                for k in range(2):
                    sp.wait_ge(st_land[k], (NST // 2) * 16)
                    sp.wait_ge(rec_land[k], landings(end + k, k))
                    sp.wait_ge(wts_land[k], landings(end + k, k))
                    sp.sem_inc(carried, 1)

            @block.vector
            def _(v_):
                V = nc.vector
                v_.sem_inc(res_ready, 2)
                v_.sem_inc(out_free, 5 if late else 4)
                for c in range(S):
                    v_.sem_inc(used[c], 2)
                v_.sem_inc(closed, 1)
                v_.sem_inc(out_ps, 1)
                v_.sem_inc(own_ps, 1)
                v_.sem_inc(fin, 1 if late else 2)
                if late:
                    v_.sem_inc(sd_ready, 1)
                V.memset(ps_h[:, 1, :], 0.0).then_inc(consts, 1)
                V.memset(ps_o[:, :], 0.0).then_inc(consts, 1)
                V.memset(ht[:, :], 0.0).then_inc(consts, 1)
                V.memset(outb[:, :, :], 0.0).then_inc(consts, 1)
                V.memset(xin[:, :, :], 0.0).then_inc(consts, 1)
                V.memset(eps[:, :], EPS).then_inc(consts, 1)
                V.memset(xres[:, :, :], 0.0).then_inc(consts, 1)
                V.memset(z[:, :, :], 0.0).then_inc(consts, 1)
                if late:
                    V.memset(mv[:, :, :], 0.0)
                    V.memset(sd[:, :], 1.0)
                V.memset(xt[:, :] if rgcn else sel[:, 0, 0, :], 0.0).then_inc(consts, 1)
                v_.wait_ge(consts, CONSTS)
                v_.wait_ge(w_in, 96 if rgcn else 32)

                def selection(v, s, c):
                    w = wts[:, s, C0 + c, 0:1]
                    if rgcn:
                        v_.wait_ge(used[c], v + 1)
                        V.tensor_scalar(sel[:, 0, c, :], iota[:, :], w, None, ALU.is_equal).then_inc(sel_sb[c], 1)
                    else:
                        v_.wait_ge(used[c], v)
                        V.tensor_scalar(sel[:, s, c, :], iota[:, :], w, None, ALU.is_equal).then_inc(sel_sb[c], 1)

                def weighted(v, s, c):
                    prods, w = ps_y[:, c % 2, :], wts[:, s, c, :]
                    v_.wait_ge(part_sb[c], v)
                    V.scalar_tensor_tensor(mid[:, c, :], prods[:, D:2 * D], w[:, 2:3], part[:, c, :],
                                           ALU.mult, ALU.add).then_inc(mid_sb[c], 1)
                    v_.wait_ge(mid_sb[c], v)
                    V.scalar_tensor_tensor(y[:, c, :], prods[:, 2 * D:3 * D], w[:, 3:4], mid[:, c, :],
                                           ALU.mult, ALU.add).then_inc(y_sb[c], 1)

                def round_(v, s, steps):
                    for c in range(S):
                        if rgcn:
                            weighted(v, s, c)
                        if rgcn and c < S - 1:
                            selection(v, s, c + 1)
                        elif rgcn:
                            v_.wait_ge(wts_land[1 - s], landings(v + 1, 1 - s))
                            selection(v + 1, 1 - s, 0)
                        for f in steps[c] if c < len(steps) else []:
                            f()
                        if not rgcn:
                            if c == 0:
                                v_.wait_ge(wts_land[1 - s], landings(v + 1, 1 - s))
                            selection(v + 1, 1 - s, c)

                def blocks(a):
                    return [a[:, b * D:b * D + D] for b in range(NB)]

                def finish(h, one):
                    dst, xr, zz = outb[:, h, :], xres[:, h, :], z[:, h if late else 0, :]
                    sq, di = ([sc[:, h, b, i:i + 1] for b in range(NB)] for i in (1, 2))

                    def after(i):
                        v_.wait_ge(fin_links[i], one)

                    def take():
                        v_.wait_ge(out_ps, one)
                        v_.wait_ge(sc_sb, one)
                        if rgcn and not last:
                            v_.wait_ge(out_free, one)
                            V.tensor_scalar(dst, ps_o[:, :], 0.0, None, ALU.max).then_inc(out_read, 1)
                            v_.wait_ge(out_read, one)
                            v_.sem_inc(fin, 1)
                        elif rgcn:
                            v_.wait_ge(res_ready, one)
                            V.tensor_tensor(zz, ps_o[:, :], xr, ALU.add).then_inc(out_read, 1)
                        else:
                            if not late:
                                v_.wait_ge(fin, one + 1)
                            for b in range(NB):
                                ins = V.scalar_tensor_tensor(blocks(za)[b], blocks(ps_o)[b], di[b], brow[:, :], ALU.mult, ALU.add)
                            ins.then_inc(out_read, 1)

                    def rows_out():
                        v_.wait_ge(out_read, one)
                        v_.wait_ge(out_free, one)
                        for b in range(NB):
                            ins = V.tensor_scalar(blocks(dst)[b], blocks(za)[b], 0.0, di[b], ALU.max, ALU.mult)
                        ins.then_inc(fin, 1)

                    def add_residual():
                        v_.wait_ge(res_ready, one)
                        v_.wait_ge(fin, one)
                        v_.wait_ge(relu_sb, one)
                        for b in range(NB):
                            ins = V.scalar_tensor_tensor(blocks(zz)[b], blocks(xr)[b], sq[b], blocks(zb)[b], ALU.mult, ALU.add)
                        ins.then_inc(fin_links[1], 1)

                    def statistics():
                        if rgcn:
                            v_.wait_ge(out_read, one)
                        else:
                            after(1)
                        v_.sem_inc(res_read, 1)
                        for b in range(NB):
                            ins = V.bn_stats(stats[:, b, :], blocks(zz)[b])
                        ins.then_inc(fin_links[2], 1)

                    def variance():
                        after(2)
                        v_.sem_inc(passed, 1)
                        for b in range(NB):
                            ins = V.bn_aggr(mv[:, b, :], stats[:, b, :])
                        ins.then_inc(var_ready, 1)

                    def inverse():
                        v_.wait_ge(sd_ready, one)
                        if late:
                            v_.wait_ge(fin, one)
                            V.reciprocal(rs[:, :], sd[:, :]).then_inc(fin_links[3], 1)
                            after(3)
                            V.scalar_tensor_tensor(shift[:, :], mv[:, :, 0], -1.0, rs[:, :], ALU.mult, ALU.mult) \
                                .then_inc(fin_links[4], 1)
                            return
                        V.reciprocal(rs[:, :], sd[:, :]).then_inc(fin_links[3], 1)
                        after(3)
                        V.tensor_tensor(rs2[:, :], rs[:, :], sc[:, h, :, 2], ALU.mult).then_inc(fin_links[4], 1)

                    def normalize():
                        after(4)
                        v_.wait_ge(out_free, one)
                        for b in range(NB):
                            ins = V.tensor_scalar(blocks(dst)[b], blocks(zz)[b], mv[:, b, 0:1], rs2[:, b:b + 1],
                                                  ALU.subtract, ALU.mult)
                        ins.then_inc(fin, 1)

                    if rgcn:
                        return [[], [take], [statistics], [variance], [], [inverse, normalize]] if last else [[], [], [take]]
                    return [[take, inverse], [add_residual, statistics], [variance]] if late else [[take], [rows_out]]

                v_.wait_ge(wts_land[0], 16)
                for c in range(1 if rgcn else S):
                    selection(1, 0, c)
                def strip(pair, h, v, more):
                    round_(v, h, finish(h, pair * 2 + (h + 1)))
                    further_rounds(v_, sh, v, more, h, lambda u, s: round_(u, s, []))

                each_strip(v_, sh, bounds, 0, NST // 2, strip)
                for j in (NST, NST + 1):
                    if late:
                        v_.wait_ge(var_ready, j)
                    else:
                        v_.wait_ge(fin, j + 2)
                    for step in finish(j % 2, j + 1):
                        for f in step:
                            f()
                if late:
                    inverse = finish(0, NST + 3)[0][1]
                    inverse()

            @block.scalar
            def _(act):
                C = nc.scalar
                act.wait_ge(consts, CONSTS)

                def turned_copy(v, c):
                    act.wait_ge(xt_ps[c], v)
                    C.activation(turned[:, c, :], ps_xt[:, c % 2, 0:P], ACT.Copy).then_inc(xt_sb[c], 1)

                def first_part(v, s, c):
                    act.wait_ge(y_ps[c], v)
                    C.activation(part[:, c, :], ps_y[:, c % 2, 0:D], ACT.Copy, scale=wts[:, s, c, 1:2]).then_inc(part_sb[c], 1)

                def node_scales(j, h):
                    act.wait_ge(fin, j + 1)
                    C.activation(sc[:, h, :, :], scales[:, bass.ds(j * NB, NB), :], ACT.Copy).then_inc(sc_sb, 1)

                def own_rows(j, h, x16, part_):
                    if part_ == 0:
                        act.wait_ge(sc_sb, j + 1)
                        act.wait_ge(in_land[h], x16)
                        act.wait_ge(own_ps, j + 1)
                    for b in range(part_ * NB // 2, (part_ + 1) * NB // 2):
                        ins = C.activation(xc[:, b * D:b * D + D], xin[:, h, b * D:b * D + D], ACT.Copy, scale=sc[:, h, b, 0:1])
                    if part_ == 1:
                        ins.then_inc(xc_sb, 1)

                def own_turned(j):
                    act.wait_ge(own_ps, j + 2)
                    C.activation(xt[:, :], ps_x[:, :], ACT.Copy).then_inc(own_sb, 1)

                def hidden(j, h):
                    act.wait_ge(out_ps, j + 1)
                    act.wait_ge(closed, j + 1)
                    C.activation(ht[:, :], ps_h[:, 1 - h, :], ACT.Copy).then_inc(ht_sb, 1)

                def deviation(j):
                    act.wait_ge(var_ready, j + 1)
                    C.activation(sd[:, :], mv[:, :, 1], ACT.Sqrt, bias=eps[:, 0:1]).then_inc(sd_ready, 1)

                def relu(j):
                    act.wait_ge(out_read, j + 1)
                    C.activation(zb[:, :], za[:, :], ACT.Relu).then_inc(relu_sb, 1)

                def normalize(j, h):
                    act.wait_ge(fin_links[4], j + 1)
                    act.wait_ge(out_free, j + 1)
                    for b in range(NB):
                        ins = C.activation(outb[:, 1 - h, b * D:b * D + D], z[:, 1 - h, b * D:b * D + D], ACT.Identity,
                                           bias=shift[:, b:b + 1], scale=rs[:, b:b + 1])
                    ins.then_inc(fin, 1)

                def round_(v, s, nxt, j=None, x16=None):
                    for c in range(S):
                        if rgcn:
                            u, cc = (v, c + 2) if c + 2 < S else (nxt, c + 2 - S)
                            turned_copy(u, cc)
                            if c == S - 1:
                                act.wait_ge(wts_land[1 - s], landings(nxt, 1 - s))
                                first_part(nxt, 1 - s, 0)
                            else:
                                first_part(v, s, c + 1)
                        if j is None:
                            continue
                        if rgcn and c == 0:
                            node_scales(j, s)
                            hidden(j, s)
                        if rgcn and c in (1, 2):
                            own_rows(j, s, x16, c - 1)
                        if not rgcn and c == 0:
                            node_scales(j, s)
                            hidden(j, s)
                            if late:
                                relu(j)
                                normalize(j, s)
                        if rgcn and c == 4:
                            own_turned(j)
                        if last and c == (4 if rgcn else 1):
                            deviation(j)

                if rgcn:
                    turned_copy(1, 0)
                    turned_copy(1, 1)
                    act.wait_ge(wts_land[0], 16)
                    first_part(1, 0, 0)
                def strip(pair, h, v, more):
                    round_(v, h, v + 1, pair * 2 + h, pair * 16 + 16)
                    further_rounds(act, sh, v, more, h, lambda u, s: round_(u, s, u + 1))

                if rgcn:
                    each_strip(act, sh, bounds, 0, NST // 2, strip)
                else:
                    with act.Fori(0, NST // 2) as pair:
                        for h in range(2):
                            round_(None, h, None, pair * 2 + h, None)
                node_scales(NST, 0)
                if late:
                    relu(NST)
                hidden(NST, 0)
                if late:
                    normalize(NST, 0)
                if last:
                    deviation(NST)
                node_scales(NST + 1, 1)
                if late:
                    relu(NST + 1)
                    normalize(NST + 1, 1)
                if last:
                    deviation(NST + 1)
                if late:
                    normalize(NST + 2, 0)

            @block.tensor
            def _(pe):
                M = nc.tensor
                pe.wait_ge(w_in, 96 if rgcn else 32)
                pe.wait_ge(consts, CONSTS)

                def turn_tile(v, s, c):
                    pe.wait_ge(landed[s][c], landings(v, s))
                    M.transpose(ps_xt[:, c % 2, 0:P], xg[:, s, c, :], ident[:, :]).then_inc(xt_ps[c], 1)

                def product(v, c):
                    pe.wait_ge(xt_sb[c], v)
                    M.matmul(ps_y[:, c % 2, 0:TRI * D], turned[:, c, :], wall_of(c), start=True, stop=True).then_inc(y_ps[c], 1)

                def wall_of(c):
                    off = (c // NG * R + c % NG * TRI) * D
                    return wall[:, off:off + TRI * D]

                def own_turn(j):
                    pe.wait_ge(xc_sb, j + 1)
                    for b in range(NB):
                        ins = M.transpose(ps_x[:, b * P:b * P + P], xc[:, b * D:b * D + D], ident[:, :])
                    ins.then_inc(own_ps, 1)

                def out(j):
                    pe.wait_ge(ht_sb, j + 1)
                    pe.wait_ge(out_read, j + 1)
                    for b in range(NB):
                        dst, hb = ps_o[:, b * D:b * D + D], ht[:, b * P:b * P + P]
                        ins = M.transpose(dst, hb, ident[:, :]) if rgcn else M.matmul(dst, hb, wgcn[:, :], start=True, stop=True)
                    ins.then_inc(out_ps, 1)

                def close(j, h, x16):
                    acc = ps_h[:, h, :]
                    if rgcn:
                        pe.wait_ge(own_sb, j + 1)
                        pe.wait_ge(cb_land[h], x16)
                        M.matmul(acc, ball[:, :], cb[:, h, :], start=False, stop=False)
                        M.matmul(acc, wself[:, :], xt[:, :], start=False, stop=True).then_inc(closed, 1)
                    else:
                        pe.wait_ge(in_land[h], x16)
                        for b in range(NB):
                            ins = M.matmul(acc[:, b * P:b * P + P], xin[:, h, b * D:b * D + D], ident[:, :],
                                           start=False, stop=b == NB - 1)
                        ins.then_inc(closed, 1)

                def round_(v, s, nxt, h, j=None, x16=None):
                    for c in range(S):
                        if rgcn:
                            u, us, cc = (v, s, c + 2) if c + 2 < S else (nxt, 1 - s, c + 2 - S)
                            turn_tile(u, us, cc)
                            u, cc = (v, c + 1) if c + 1 < S else (nxt, 0)
                            product(u, cc)
                            pe.wait_ge(y_sb[c], v)
                            lhs, selected = y[:, c, :], sel[:, 0, c, :]
                        else:
                            pe.wait_ge(landed[s][c], landings(v, s))
                            pe.wait_ge(sel_sb[c], v)
                            lhs, selected = xg[:, s, c, :], sel[:, s, c, :]
                        M.matmul(ps_h[:, h, :], lhs, selected, start=j is not None and c == 0, stop=False).then_inc(used[c], 1)
                        if j is None:
                            continue
                        if rgcn and c == 4:
                            own_turn(j)
                        if c == S - 1:
                            out(j)

                if rgcn:
                    turn_tile(1, 0, 0)
                    turn_tile(1, 0, 1)
                    product(1, 0)
                def strip(pair, h, v, more):
                    x16 = pair * 16 + 16
                    round_(v, h, v + 1, h, pair * 2 + h, x16)
                    further_rounds(pe, sh, v, more, h, lambda u, s: round_(u, s, u + 1, h))
                    close(pair * 2 + h, h, x16)

                each_strip(pe, sh, bounds, 0, NST // 2, strip)
                out(NST)
        clear(nc, sems)


def program(nc, x, src, dst, edge_type, w0, b0, w1, b1, w2, b2, out, dram):
    sh = Shapes(x.shape[0], src.shape[0])
    assert sh.NST % 2 == 0 and sh.N % NB == 0 and sh.NST >= 10
    with ExitStack() as ctx:
        def t(name, shape, dt=FP32):
            return ctx.enter_context(nc.sbuf_tensor(name, shape, dt))

        def landings_of(stage, tiles):
            return [[ctx.enter_context(nc.semaphore(f"{stage}_landed{s}_{c}")) for c in range(tiles)] for s in range(2)]

        res = {
            "iota": t("iota", [P, STRIP]),
            "ident": t("ident", [P, P]),
            "bounds": t("bounds", [P, 2, sh.NST + 1], I32),
            "scales": t("scales", [P, (sh.NST + 2) * NB, 3]),
            "landed": {"s": [ctx.enter_context(nc.semaphore(f"s_landed{k}")) for k in range(2)],
                       "a1": landings_of("a1", SLOTS), "a2": landings_of("a2", SLOTS),
                       "g1": landings_of("g1", NG), "g2": landings_of("g2", NG)},
        }
        build_tables(nc, sh, src, dst, edge_type, dram, res)
        build_coefs(nc, sh, dram, res)
        layer(nc, sh, "a1", True, False, x, x, None, dram["h1"], w0[0], b0[0], dram, res)
        layer(nc, sh, "a2", True, True, dram["h1"], dram["h1"], x, dram["x1"], w0[1], b0[1], dram, res)
        layer(nc, sh, "g1", False, False, dram["x1"], dram["x1"], None, dram["hs"], w1, b1, dram, res)
        layer(nc, sh, "g2", False, True, dram["hs"], dram["hs"], dram["x1"], out, w2, b2, dram, res)


_INS = ["x", "src", "dst", "edge_type_9", "L0_gnn_rgcn_weights", "L0_gnn_rgcn_biases",
        "L1_gnn_W1", "L1_gnn_b1", "L1_gnn_W2", "L1_gnn_b2"]


def kernel(**inputs):
    import numpy as np
    import concourse.bacc as bacc
    from concourse.bass_utils import run_bass_kernel_spmd

    nc = bacc.Bacc("TRN2", target_bir_lowering=False, num_devices=1)
    arrays, args = {}, []
    for name in _INS:
        a = np.ascontiguousarray(inputs[name])
        arrays["in_" + name] = a
        args.append(nc.dram_tensor("in_" + name, a.shape, mybir.dt.from_np(a.dtype), kind="ExternalInput").ap())
    n, e = inputs["x"].shape[0], inputs["src"].shape[0]
    sh = Shapes(n, e)
    dram = {
        "table": nc.dram_tensor("dram_table", (sh.NR * P * SLOTS, WORDS), FP32, kind="Internal").ap(),
        "weights": nc.dram_tensor("dram_weights", (sh.NR * P * SLOTS, 1 + TRI), FP32, kind="Internal").ap(),
        "cbt": nc.dram_tensor("dram_cbt", (sh.NST, KK + 1, STRIP), FP32, kind="Internal").ap(),
        "h1": nc.dram_tensor("dram_h1", (sh.NST * STRIP, D), FP32, kind="Internal").ap(),
        "x1": nc.dram_tensor("dram_x1", (sh.NST * STRIP, D), FP32, kind="Internal").ap(),
        "hs": nc.dram_tensor("dram_hs", (sh.NST * STRIP, D), FP32, kind="Internal").ap(),
    }
    out = nc.dram_tensor("out", (n, D), FP32, kind="ExternalOutput").ap()
    program(nc, *args, out, dram)
    r = run_bass_kernel_spmd(nc, [arrays], core_ids=[0])
    return r.results[0]["out"]
```
